# Optimizing a Trainium2 kernel written in Bass

```python
import numpy as np
import jax
import jax.numpy as jnp

def _softmax(x, axis=-1):
    return jax.nn.softmax(x, axis=axis)

def _gelu(x):
    return jax.nn.gelu(x, approximate=True)

def _silu(x):
    return jax.nn.silu(x)

def _sigmoid(x):
    return jax.nn.sigmoid(x)

def _layernorm(x, axis=-1, eps=1e-05):
    m = jnp.mean(x, axis=axis, keepdims=True)
    v = jnp.var(x, axis=axis, keepdims=True)
    return (x - m) / jnp.sqrt(v + eps)

def _scatter_add(tgt, idx, src, axis=0):
    return tgt.at[idx].add(src)

def _segment_sum(src, seg, n):
    return jax.ops.segment_sum(src, seg, n)
kernel_name = 'mk_macaron_d2_jaxref_r8_d0eea1'

def setup_inputs(seed: int=0):
    np.random.seed(seed)
    _w = jnp.asarray

    def _L0_attn_setup():
        import jax, jax.numpy as jnp
        import numpy as np
        H = 128
        NH = 16
        HD = H // NH
        BETA = 1.0
        STEPS = 2
        EPS_NORM = 1e-12
        EPS_LN = 1e-05

        def _l2norm(x):
            n = jnp.linalg.norm(x, axis=-1, keepdims=True)
            return x / jnp.maximum(n, EPS_NORM)
        key = jax.random.key(seed)
        ks = jax.random.split(key, 10)
        s = 1.0 / np.sqrt(H)
        return {'hidden_states': jax.random.normal(ks[0], (2, 256, H), jnp.float32), 'Wq': jax.random.normal(ks[1], (H, H), jnp.float32) * s, 'bq': jnp.zeros((H,), jnp.float32), 'Wk': jax.random.normal(ks[2], (H, H), jnp.float32) * s, 'bk': jnp.zeros((H,), jnp.float32), 'Wv': jax.random.normal(ks[3], (H, H), jnp.float32) * s, 'bv': jnp.zeros((H,), jnp.float32), 'Wo': jax.random.normal(ks[4], (H, H), jnp.float32) * s, 'bo': jnp.zeros((H,), jnp.float32), 'ln_w': jnp.ones((H,), jnp.float32), 'ln_b': jnp.zeros((H,), jnp.float32)}
    _L0_attn_in = _L0_attn_setup()

    def _L0_ffn_setup():
        import jax, jax.numpy as jnp
        import numpy as np
        key = jax.random.key(seed)
        k1, k2, k3, k4, k5 = jax.random.split(key, 5)
        d_in, d_out, r = (128, 128, 32)
        x = jax.random.normal(k1, (8, 1024, d_in), dtype=jnp.float32)
        W = jax.random.normal(k2, (d_out, d_in), dtype=jnp.float32) * (1.0 / np.sqrt(d_in))
        b = jax.random.normal(k3, (d_out,), dtype=jnp.float32) * 0.01
        V_r = jax.random.normal(k4, (d_in, r), dtype=jnp.float32) * (1.0 / np.sqrt(d_in))
        C = jax.random.normal(k5, (d_out, r), dtype=jnp.float32) * (1.0 / np.sqrt(r))
        return {'x': x, 'W': W, 'b': b, 'V_r': V_r, 'C': C}
    _L0_ffn_in = _L0_ffn_setup()

    def _L1_attn_setup():
        import jax, jax.numpy as jnp
        import numpy as np
        import math
        DIM = 128
        NUM_HEADS = 16
        HEAD_DIM = DIM // NUM_HEADS
        BLOCK_SIZE = 64

        def _block_mask(src_blocks, tgt_blocks, num_blocks):
            i = jnp.arange(num_blocks)[:, None]
            j = jnp.arange(num_blocks)[None, :]
            band = jnp.abs(i - j) <= 1
            glob = (j == 0) | (j == num_blocks - 1)
            bm = band | glob
            bm = bm.at[src_blocks, tgt_blocks].set(True)
            return bm
        key = jax.random.key(seed)
        ks = jax.random.split(key, 12)
        B, S = (2, 256)
        x = jax.random.normal(ks[0], (B, S, DIM), dtype=jnp.float32)
        scale = 0.02
        Wq = jax.random.normal(ks[1], (DIM, DIM), dtype=jnp.float32) * scale
        bq = jnp.zeros((DIM,), dtype=jnp.float32)
        Wk = jax.random.normal(ks[2], (DIM, DIM), dtype=jnp.float32) * scale
        bk = jnp.zeros((DIM,), dtype=jnp.float32)
        Wv = jax.random.normal(ks[3], (DIM, DIM), dtype=jnp.float32) * scale
        bv = jnp.zeros((DIM,), dtype=jnp.float32)
        Wo = jax.random.normal(ks[4], (DIM, DIM), dtype=jnp.float32) * scale
        bo = jnp.zeros((DIM,), dtype=jnp.float32)
        num_blocks = S // BLOCK_SIZE
        src_blocks = jax.random.randint(ks[5], (3,), 0, num_blocks, dtype=jnp.int32)
        tgt_blocks = jax.random.randint(ks[6], (3,), 0, num_blocks, dtype=jnp.int32)
        return {'x': x, 'Wq': Wq, 'bq': bq, 'Wk': Wk, 'bk': bk, 'Wv': Wv, 'bv': bv, 'Wo': Wo, 'bo': bo, 'src_blocks': src_blocks, 'tgt_blocks': tgt_blocks}
    _L1_attn_in = _L1_attn_setup()

    def _L1_ffn_setup():
        import jax, jax.numpy as jnp
        import numpy as np
        DIM = 128
        HIDDEN = 128
        NUM_EXPERTS = 8
        TOP_K = 2
        key = jax.random.key(seed)
        ks = jax.random.split(key, 8)
        std = 0.02
        x = jax.random.normal(ks[0], (2, 128, DIM), dtype=jnp.float32)
        gate_w = jax.random.normal(ks[1], (NUM_EXPERTS, DIM), dtype=jnp.float32) * std
        w1 = jax.random.normal(ks[2], (NUM_EXPERTS, DIM, HIDDEN), dtype=jnp.float32) * std
        w2 = jax.random.normal(ks[3], (NUM_EXPERTS, HIDDEN, DIM), dtype=jnp.float32) * std
        w3 = jax.random.normal(ks[4], (NUM_EXPERTS, DIM, HIDDEN), dtype=jnp.float32) * std
        w1s = jax.random.normal(ks[5], (1, DIM, HIDDEN), dtype=jnp.float32) * std
        w2s = jax.random.normal(ks[6], (1, HIDDEN, DIM), dtype=jnp.float32) * std
        w3s = jax.random.normal(ks[7], (1, DIM, HIDDEN), dtype=jnp.float32) * std
        return {'x': x, 'gate_w': gate_w, 'w1': w1, 'w2': w2, 'w3': w3, 'w1s': w1s, 'w2s': w2s, 'w3s': w3s}
    _L1_ffn_in = _L1_ffn_setup()
    _d = {'L0_attn_hidden_states': _L0_attn_in['hidden_states'], 'L0_attn_Wq': _L0_attn_in['Wq'], 'L0_attn_bq': _L0_attn_in['bq'], 'L0_attn_Wk': _L0_attn_in['Wk'], 'L0_attn_bk': _L0_attn_in['bk'], 'L0_attn_Wv': _L0_attn_in['Wv'], 'L0_attn_bv': _L0_attn_in['bv'], 'L0_attn_Wo': _L0_attn_in['Wo'], 'L0_attn_bo': _L0_attn_in['bo'], 'L0_attn_ln_w': _L0_attn_in['ln_w'], 'L0_attn_ln_b': _L0_attn_in['ln_b'], 'L0_ffn_W': _L0_ffn_in['W'], 'L0_ffn_b': _L0_ffn_in['b'], 'L0_ffn_V_r': _L0_ffn_in['V_r'], 'L0_ffn_C': _L0_ffn_in['C'], 'L1_attn_Wq': _L1_attn_in['Wq'], 'L1_attn_bq': _L1_attn_in['bq'], 'L1_attn_Wk': _L1_attn_in['Wk'], 'L1_attn_bk': _L1_attn_in['bk'], 'L1_attn_Wv': _L1_attn_in['Wv'], 'L1_attn_bv': _L1_attn_in['bv'], 'L1_attn_Wo': _L1_attn_in['Wo'], 'L1_attn_bo': _L1_attn_in['bo'], 'L1_attn_src_blocks': _L1_attn_in['src_blocks'], 'L1_attn_tgt_blocks': _L1_attn_in['tgt_blocks'], 'L1_ffn_gate_w': _L1_ffn_in['gate_w'], 'L1_ffn_w1': _L1_ffn_in['w1'], 'L1_ffn_w2': _L1_ffn_in['w2'], 'L1_ffn_w3': _L1_ffn_in['w3'], 'L1_ffn_w1s': _L1_ffn_in['w1s'], 'L1_ffn_w2s': _L1_ffn_in['w2s'], 'L1_ffn_w3s': _L1_ffn_in['w3s']}
    _x0 = _d['L0_attn_hidden_states']
    _d['L0_attn_hidden_states'] = jax.random.normal(jax.random.fold_in(jax.random.key(seed), 1), (16, 512, 128), dtype=_x0.dtype)
    del _x0
    return _d

def reference(L0_attn_hidden_states, L0_attn_Wq, L0_attn_bq, L0_attn_Wk, L0_attn_bk, L0_attn_Wv, L0_attn_bv, L0_attn_Wo, L0_attn_bo, L0_attn_ln_w, L0_attn_ln_b, L0_ffn_W, L0_ffn_b, L0_ffn_V_r, L0_ffn_C, L1_attn_Wq, L1_attn_bq, L1_attn_Wk, L1_attn_bk, L1_attn_Wv, L1_attn_bv, L1_attn_Wo, L1_attn_bo, L1_attn_src_blocks, L1_attn_tgt_blocks, L1_ffn_gate_w, L1_ffn_w1, L1_ffn_w2, L1_ffn_w3, L1_ffn_w1s, L1_ffn_w2s, L1_ffn_w3s):

    def _L0_attn_ref(hidden_states, Wq, bq, Wk, bk, Wv, bv, Wo, bo, ln_w, ln_b):
        import jax, jax.numpy as jnp
        import numpy as np
        H = 128
        NH = 16
        HD = H // NH
        BETA = 1.0
        STEPS = 2
        EPS_NORM = 1e-12
        EPS_LN = 1e-05

        def _l2norm(x):
            n = jnp.linalg.norm(x, axis=-1, keepdims=True)
            return x / jnp.maximum(n, EPS_NORM)
        B, S, _ = hidden_states.shape
        residual = hidden_states
        mu = jnp.mean(hidden_states, axis=-1, keepdims=True)
        var = jnp.mean(jnp.square(hidden_states - mu), axis=-1, keepdims=True)
        x = (hidden_states - mu) * jax.lax.rsqrt(var + EPS_LN) * ln_w + ln_b
        q = (x @ Wq + bq).reshape(B, S, NH, HD)
        k = (x @ Wk + bk).reshape(B, S, NH, HD)
        v = (x @ Wv + bv).reshape(B, S, NH, HD)
        q = _l2norm(q)
        k = _l2norm(k)
        state = q
        for _ in range(STEPS):
            sim = jnp.einsum('bqhd,bkhd->bqhk', state, k)
            att = jax.nn.softmax(BETA * sim, axis=-1)
            state = jnp.einsum('bqhk,bkhd->bqhd', att, v)
        o = state.reshape(B, S, H) @ Wo + bo
        return residual + o

    def _L0_ffn_ref(x, W, b, V_r, C):
        import jax, jax.numpy as jnp
        import numpy as np
        base = jnp.einsum('bsd,od->bso', x, W) + b
        correction = jnp.einsum('bsr,or->bso', jnp.einsum('bsd,dr->bsr', x, V_r), C)
        return base + correction

    def _L1_attn_ref(x, Wq, bq, Wk, bk, Wv, bv, Wo, bo, src_blocks, tgt_blocks):
        import jax, jax.numpy as jnp
        import numpy as np
        import math
        DIM = 128
        NUM_HEADS = 16
        HEAD_DIM = DIM // NUM_HEADS
        BLOCK_SIZE = 64

        def _block_mask(src_blocks, tgt_blocks, num_blocks):
            i = jnp.arange(num_blocks)[:, None]
            j = jnp.arange(num_blocks)[None, :]
            band = jnp.abs(i - j) <= 1
            glob = (j == 0) | (j == num_blocks - 1)
            bm = band | glob
            bm = bm.at[src_blocks, tgt_blocks].set(True)
            return bm
        B, S, _ = x.shape
        nb = S // BLOCK_SIZE
        q = (x @ Wq.T + bq).reshape(B, NUM_HEADS, S, HEAD_DIM)
        k = (x @ Wk.T + bk).reshape(B, NUM_HEADS, S, HEAD_DIM)
        v = (x @ Wv.T + bv).reshape(B, NUM_HEADS, S, HEAD_DIM)
        bm = _block_mask(src_blocks, tgt_blocks, nb)
        mask = jnp.repeat(jnp.repeat(bm, BLOCK_SIZE, axis=0), BLOCK_SIZE, axis=1)
        scores = jnp.einsum('bhqd,bhkd->bhqk', q, k) / math.sqrt(HEAD_DIM)
        scores = jnp.where(mask[None, None], scores, jnp.float32(-1000000000.0))
        attn = jax.nn.softmax(scores, axis=-1)
        out = jnp.einsum('bhqk,bhkd->bhqd', attn, v)
        out = out.transpose(0, 2, 1, 3).reshape(B, S, DIM)
        return out @ Wo.T + bo

    def _L1_ffn_ref(x, gate_w, w1, w2, w3, w1s, w2s, w3s):
        import jax, jax.numpy as jnp
        import numpy as np
        DIM = 128
        HIDDEN = 128
        NUM_EXPERTS = 8
        TOP_K = 2
        bs, slen, dim = x.shape
        xt = x.reshape(bs * slen, dim)
        logits = xt @ gate_w.T
        scores = jax.nn.softmax(logits.astype(jnp.float32), axis=1).astype(x.dtype)
        top_scores, sel = jax.lax.top_k(scores, TOP_K)
        sel_flat = sel.reshape(-1)
        order = jnp.argsort(sel_flat, stable=True)
        top_scores_sorted = top_scores.reshape(-1)[order]
        token_idx = order // TOP_K
        eid = sel_flat[order]
        routed_in = xt[token_idx] * top_scores_sorted[:, None]
        out_routed = jnp.zeros_like(routed_in)
        for e in range(NUM_EXPERTS):
            m = (eid == e)[:, None]
            xe = jnp.where(m, routed_in, 0.0)
            h = jax.nn.silu(xe @ w1[e]) * (xe @ w3[e])
            out_routed = out_routed + jnp.where(m, h @ w2[e], 0.0)
        hs = jax.nn.silu(xt @ w1s[0]) * (xt @ w3s[0])
        out = hs @ w2s[0]
        out = out.at[token_idx].add(out_routed)
        return out.reshape(bs, slen, dim)
    x = L0_attn_hidden_states
    x = x + 0.5 * _L0_ffn_ref(_layernorm(x, axis=-1), L0_ffn_W, L0_ffn_b, L0_ffn_V_r, L0_ffn_C)
    x = x + _L0_attn_ref(_layernorm(x, axis=-1), L0_attn_Wq, L0_attn_bq, L0_attn_Wk, L0_attn_bk, L0_attn_Wv, L0_attn_bv, L0_attn_Wo, L0_attn_bo, L0_attn_ln_w, L0_attn_ln_b)
    x = x + 0.5 * _L0_ffn_ref(_layernorm(x, axis=-1), L0_ffn_W, L0_ffn_b, L0_ffn_V_r, L0_ffn_C)
    x = x + 0.5 * _L1_ffn_ref(_layernorm(x, axis=-1), L1_ffn_gate_w, L1_ffn_w1, L1_ffn_w2, L1_ffn_w3, L1_ffn_w1s, L1_ffn_w2s, L1_ffn_w3s)
    x = x + _L1_attn_ref(_layernorm(x, axis=-1), L1_attn_Wq, L1_attn_bq, L1_attn_Wk, L1_attn_bk, L1_attn_Wv, L1_attn_bv, L1_attn_Wo, L1_attn_bo, L1_attn_src_blocks, L1_attn_tgt_blocks)
    x = x + 0.5 * _L1_ffn_ref(_layernorm(x, axis=-1), L1_ffn_gate_w, L1_ffn_w1, L1_ffn_w2, L1_ffn_w3, L1_ffn_w1s, L1_ffn_w2s, L1_ffn_w3s)
    return x

_drawn_inputs = setup_inputs


def setup_inputs(seed=0):
    import zlib

    import numpy as np

    out = dict(_drawn_inputs(seed))
    spreads = {'L0_attn_bq': (0.0, 2.0),
     'L0_attn_bk': (0.0, 2.0),
     'L0_attn_bv': (0.0, 0.1),
     'L0_attn_bo': (0.0, 0.1),
     'L0_attn_ln_w': (1.0, 0.6),
     'L0_attn_ln_b': (0.0, 0.1),
     'L1_attn_bq': (0.0, 0.8),
     'L1_attn_bk': (0.0, 0.8),
     'L1_attn_bv': (0.0, 0.8),
     'L1_attn_bo': (0.0, 0.301)}
    factors = {'L0_attn_Wq': 8.0,
     'L0_attn_Wk': 7.419,
     'L0_ffn_b': 8.0,
     'L1_attn_Wq': 8.0,
     'L1_attn_Wk': 8.0,
     'L1_attn_Wv': 8.0,
     'L1_attn_Wo': 8.0,
     'L1_ffn_gate_w': 8.0,
     'L1_ffn_w1': 8.0,
     'L1_ffn_w2': 8.0,
     'L1_ffn_w3': 8.0,
     'L1_ffn_w1s': 8.0,
     'L1_ffn_w2s': 8.0,
     'L1_ffn_w3s': 8.0}
    for name, (base, spread) in spreads.items():
        noise = np.random.default_rng([zlib.crc32(name.encode()), seed]).standard_normal(out[name].shape)
        drawn = base * np.exp(spread * noise) if base else spread * noise
        out[name] = jnp.asarray(drawn.astype(out[name].dtype))
    for name, factor in factors.items():
        out[name] = (out[name] * factor).astype(out[name].dtype)
    return out
```

```python
from contextlib import ExitStack

import numpy as np

import concourse.bass as bass
from concourse import mybir

F32 = mybir.dt.float32
F32R = mybir.dt.float32r
I32 = mybir.dt.int32
U32 = mybir.dt.uint32
ALU = mybir.AluOpType
ACT = mybir.ActivationFunctionType
AX_X = mybir.AxisListType.X

P = 128
NB = 16
S = 512
TC = S // P
NH = 16
HD = P // NH
NG = 4
ROWS = 32
NE = 8
PAIRS = 5
MASK_BLOCK = 64
NJ = S // MASK_BLOCK
TOKENS_OF_BLOCK = MASK_BLOCK // NH
EPS = 1e-5
RSQRT_GUESS = float(0x5F3759DF)

B_ST = 0
B_SM = 4
B_UT = 6
B_TP = 7
B_OUT = 5

ADD0 = 3 * HD


def signals(nc, ctx, prefix, names):
    return {n: ctx.enter_context(nc.semaphore(f"{prefix}_{n}")) for n in names.split()}


FFN_SIGNALS = "ln_ready xt_psum xt_ready y_ready xb_ready"
MOE_SIGNALS = ("ln_ready xt_psum xt_ready logits_ready shifted exped gates_ready gu_ready tanh_ready "
               "h_ready ht_ready ht_copied mm2_done acc_ready acc_read")
ATTN_SIGNALS = ("x1_ready ln_ready xt_psum xt_ready qkv_psum v_ready hi_ready dup_ready lo_ready op_psum "
                "op_act op_dve one_ready st_ready exp_done pv_done ut_copied sm_ready sm_read tp_full tp_read "
                "state_ready qt_ready mx_ready qm_ready o_ready ot_psum ot_ready y_ready res_ready")


def build(nc, x, ffn_wT, ffn_vT, ffn_cT, ffn_b, wqkv0, bqkv0, wo0, bo0, lnw, lnb,
          wqkv1, bqkv1, wo1, bo1, src, tgt, gateT, w13, w2, ident, consts, out):
    with ExitStack() as ctx:
        def sb(name, shape, dt=F32):
            return ctx.enter_context(nc.sbuf_tensor(name, shape, dt))

        ps = ctx.enter_context(nc.psum_tensor("ps", [P, 8, 512], F32))

        id_sb = sb("id_sb", [P, P])
        con = sb("con", [P, 25])
        weff = sb("weff", [P, P])
        vT = sb("vT", [ROWS, P])
        cT = sb("cT", [ROWS, P])
        wqkv = [sb(f"wqkv_{i}", [P, 3 * P]) for i in range(2)]
        bqkv = [sb(f"bqkv_{i}", [P, 3 * P]) for i in range(2)]
        wo = [sb(f"wo_{i}", [P, P]) for i in range(2)]
        bo = [sb(f"bo_{i}", [P, P]) for i in range(2)]
        bffn = sb("bffn", [P, P])
        lnw_sb = sb("lnw_sb", [P, 1])
        lnb_sb = sb("lnb_sb", [P, 1])
        gate_sb = sb("gate_sb", [P, NE])
        w13_sb = sb("w13_sb", [P, (NE + 1) * 2 * P])
        w2_sb = sb("w2_sb", [P, NE + 1, P])
        pairs_i = sb("pairs_i", [P, 2, 3], I32)
        pairs_f = sb("pairs_f", [P, 2, 3])
        hit = sb("hit", [P, 3, NJ])
        maskb = sb("maskb", [P, NJ])

        X = sb("X", [P, TC, P])
        R = sb("R", [P, TC, P])
        xn = sb("xn", [P, TC, P])
        xT = sb("xT", [P, S])
        O = sb("O", [P, TC, P])
        stats = sb("stats", [P, TC, 6])
        mv = sb("mv", [P, TC, 2])
        rs_v = sb("rs_v", [P, P])
        rs_y = sb("rs_y", [P, P])
        rs_t = sb("rs_t", [P, P])

        qkv = sb("qkv", [P, TC, 2 * P])
        stack0 = {"q": sb("stackq0", [P, TC * NH, ROWS]), "k": sb("stackk0", [P, TC * NH, ROWS])}
        stack1 = {"q": sb("stackq1", [P, TC * NH, ROWS]), "k": sb("stackk1", [P, TC * NH, ROWS])}
        stack1["v"] = stack0["q"]
        kpad = sb("kpad", [P, NH, S], F32R)
        qT = sb("qT", [P, NG * S], F32R)
        vT_all = sb("vT_all", [P, NG * S])
        v_sb = sb("v_sb", [P, TC, NH, ROWS])
        probs = sb("probs", [P, 2, NG, TC, S])
        uts = [sb(f"uts{i}", [P, S]) for i in range(2)]
        mx = sb("mx", [P, TC * NG, ROWS])
        negmax = sb("negmax", [P, TC, NG])
        rden = sb("rden", [P, TC * NG])
        st8 = sb("st8", [P, TC * NG, HD])

        scratch = probs[:].rearrange("p a g c s -> p (a g c s)")
        squares = scratch[:, 0:TC * 2 * P].rearrange("p (c x) -> p c x", c=TC)
        th = [scratch[:, i * 256:(i + 1) * 256] for i in range(2)]
        ga = [scratch[:, (2 + i) * 256:(3 + i) * 256] for i in range(2)]
        hb = [scratch[:, (4 + i) * 256:(5 + i) * 256] for i in range(2)]
        hT = [scratch[:, (6 + i) * 256:(7 + i) * 256] for i in range(2)]

        lmax = sb("lmax", [P, TC])
        el = sb("el", [P, TC, NE])
        pr = sb("pr", [P, TC, NE])
        top = sb("top", [P, TC, 8])
        idx = sb("idx", [P, TC, 8], U32)
        idxf = sb("idxf", [P, TC, 8])
        first = sb("first", [P, TC, NE])
        second = sb("second", [P, TC, NE])
        gate = sb("gate", [P, TC, NE + 1])
        gate_half = sb("gate_half", [P, TC, NE + 1])
        gate_sq = sb("gate_sq", [P, TC, NE + 1])

        loaded = ctx.enter_context(nc.semaphore("loaded"))
        zeroed = ctx.enter_context(nc.semaphore("zeroed"))
        prep = ctx.enter_context(nc.semaphore("prep"))
        weff_psum = ctx.enter_context(nc.semaphore("weff_psum"))
        loads = [
            (id_sb[:], ident), (con[:], consts), (weff[:], ffn_wT), (vT[:], ffn_vT), (cT[:], ffn_cT),
            (wqkv[0][:], wqkv0), (wqkv[1][:], wqkv1), (wo[0][:], wo0), (wo[1][:], wo1),
            (lnw_sb[:], lnw), (lnb_sb[:], lnb), (gate_sb[:], gateT), (w13_sb[:], w13), (w2_sb[:], w2),
            (bqkv[0][:], bqkv0.partition_broadcast(P)), (bqkv[1][:], bqkv1.partition_broadcast(P)),
            (bo[0][:], bo0.partition_broadcast(P)), (bo[1][:], bo1.partition_broadcast(P)),
            (bffn[:], ffn_b.partition_broadcast(P)),
            (pairs_i[:, 0, :], src.partition_broadcast(P)), (pairs_i[:, 1, :], tgt.partition_broadcast(P)),
        ]
        with nc.Block() as setup:
            @setup.sync
            def _(sp):
                for dst, source in loads:
                    sp.dma_start(dst, source).then_inc(loaded, 16)
                sp.wait_ge(loaded, 16 * len(loads))

            @setup.gpsimd
            def _(pool):
                zero = [stack0["q"][:], stack0["k"][:], stack1["q"][:], stack1["k"][:], v_sb[:],
                        mx[:], kpad[:].bitcast(F32), gate[:]]
                for t in zero:
                    nc.gpsimd.memset(t, 0.0).then_inc(zeroed, 1)
                pool.wait_ge(zeroed, len(zero))
                nc.gpsimd.memset(stack0["k"][:, :, ADD0:ADD0 + 1], 1.0).then_inc(zeroed, 1)
                nc.gpsimd.memset(v_sb[:, :, :, HD:HD + 1], 1.0).then_inc(zeroed, 1)
                nc.gpsimd.memset(gate[:, :, NE:NE + 1], 1.0).then_inc(zeroed, 1)

            @setup.tensor
            def _(pe):
                pe.wait_ge(loaded, 16 * len(loads))
                nc.tensor.matmul(ps[:, B_TP, 0:P], vT[:], cT[:], start=True, stop=True).then_inc(weff_psum, 1)

            @setup.vector
            def _(dve):
                n = [0]

                def link(ins):
                    n[0] += 1
                    ins.then_inc(prep, 1)
                    dve.wait_ge(prep, n[0])

                dve.wait_ge(loaded, 16 * len(loads))
                dve.wait_ge(weff_psum, 1)
                link(nc.vector.tensor_tensor(weff[:], ps[:, B_TP, 0:P], weff[:], ALU.add))
                link(nc.vector.tensor_scalar(weff[:], weff[:], 0.5, None, ALU.mult))
                link(nc.vector.tensor_scalar(bffn[:], bffn[:], 0.5, None, ALU.mult))
                scale = float(HD) ** -0.5
                link(nc.vector.tensor_scalar(wqkv[1][:, 0:P], wqkv[1][:, 0:P], scale, None, ALU.mult))
                link(nc.vector.tensor_scalar(bqkv[1][:, 0:P], bqkv[1][:, 0:P], scale, None, ALU.mult))
                link(nc.vector.tensor_copy(pairs_f[:], pairs_i[:]))
                own = con[:, 3 * NJ:3 * NJ + 1]
                for r in range(3):
                    link(nc.vector.tensor_scalar(hit[:, r, :], con[:, 2 * NJ:3 * NJ], pairs_f[:, 1, r:r + 1], None,
                                                 ALU.is_equal))
                    link(nc.vector.tensor_scalar(pairs_f[:, 0, r:r + 1], pairs_f[:, 0, r:r + 1], own, None,
                                                 ALU.is_equal))
                    link(nc.vector.tensor_scalar(hit[:, r, :], hit[:, r, :], pairs_f[:, 0, r:r + 1], None, ALU.mult))
                    link(nc.vector.tensor_tensor(maskb[:], con[:, 0:NJ] if r == 0 else maskb[:], hit[:, r, :],
                                                 ALU.max))
                link(nc.vector.tensor_scalar(maskb[:], maskb[:], -1.0, 1e9, ALU.add, ALU.mult))
                dve.wait_ge(zeroed, 8)
                link(nc.vector.tensor_copy(stack1["q"][:, :, ADD0:ROWS],
                                           maskb[:].unsqueeze(1).to_broadcast([P, TC * NH, NJ])))
                link(nc.vector.tensor_copy(stack1["k"][:, :, ADD0:ROWS],
                                           con[:, NJ:2 * NJ].unsqueeze(1).to_broadcast([P, TC * NH, NJ])))

        x_loaded = ctx.enter_context(nc.semaphore("x_loaded"))
        stored = ctx.enter_context(nc.semaphore("stored"))
        dve_step = ctx.enter_context(nc.semaphore("dve_step"))
        pool_step = ctx.enter_context(nc.semaphore("pool_step"))
        ffn = [signals(nc, ctx, f"ffn{k}", FFN_SIGNALS) for k in range(2)]
        moe = [signals(nc, ctx, f"moe{k}", MOE_SIGNALS) for k in range(2)]
        attn = [signals(nc, ctx, f"attn{k}", ATTN_SIGNALS) for k in range(2)]
        turn_seen = ctx.enter_context(nc.semaphore("turn_seen"))
        turn_end = ctx.enter_context(nc.semaphore("turn_end"))
        turn_go = ctx.enter_context(nc.semaphore("turn_go"))
        cleared = [x_loaded, stored, dve_step, pool_step] + [s for d in ffn + moe + attn for s in d.values()]

        x_dram = x.rearrange("b (c p) d -> b p c d", p=P)
        out_dram = out.rearrange("b (c p) d -> b p c d", p=P)

        WINDOWS = (2 * NG, NG)
        MAXED = (NG, 0)
        LEAD = 1
        KINDS = ("kq" * NG, "k" * NG + "q" * NG + "v" * NG)

        def stack_block(a, n):
            if a == 0:
                return [stack0[KINDS[0][n]][:, tc * NH + NG * (n // 2):tc * NH + NG * (n // 2) + NG, :]
                        for tc in range(TC)]
            return [stack1[KINDS[1][n]][:, NG * c:NG * c + NG, :] for c in range(4 * (n % NG), 4 * (n % NG) + 4)]

        def token_view(a, tile):
            if a == 0:
                return tile[:].rearrange("p (c h) e -> p c h e", c=TC)
            return tile[:].rearrange("p (h c) e -> p c h e", c=TC)

        def all_kinds(a):
            return KINDS[a] + "w" * (NG * a)

        def copies(a, n, part):
            return all_kinds(a)[n] == "k" or (n // (2 - a)) % 2 == part

        def copied(a, n, part):
            return sum(copies(a, i, part) for i in range(n))

        def operand_copies(a, n, kind, part):
            bank = ps[:, 4 + n % 4, :]
            if kind == "k":
                pairs = []
                for j in range(2 * part, 2 * part + 2):
                    rows = slice(ROWS * j, ROWS * (j + 1))
                    if a == 0:
                        pairs.append((kpad[rows, NG * j + n // 2, :], bank[rows, :]))
                    else:
                        dst = kpad[rows, NG * j:NG * j + NG, :].rearrange("r h (t c) -> r c (h t)", c=NH)
                        pairs.append((dst[:, 4 * n:4 * n + 4, :], bank[rows, :].rearrange("r (c x) -> r c x", c=4)))
                return pairs
            if kind == "w":
                g = n % 4
                dst = v_sb[:, :, NG * g:NG * g + NG, :].rearrange("p c j e -> p c (j e)")
                return [(dst, bank.rearrange("p (c x) -> p c x", c=TC))]
            if a == 0:
                return [(qT[:, (n // 2) * S:(n // 2 + 1) * S], bank)]
            tile = qT if kind == "q" else vT_all
            dst = tile[:].rearrange("p (x c) -> p c x", c=NH)
            c0 = 4 * (n % NG)
            return [(dst[:, c0:c0 + 4, :], bank.rearrange("p (c x) -> p c x", c=4))]

        block = ctx.enter_context(nc.Block())

        @block.sync
        def _(sp):
            with sp.Fori(0, NB) as b:
                sp.dma_start(X[:], x_dram[b]).then_inc(x_loaded, 16)
                sp.wait_ge(moe[1]["acc_read"], TC)
                sp.dma_start(out_dram[b], X[:]).then_inc(stored, 16)
                sp.wait_ge(stored, 16)
                sp.wait_ge(turn_end, (b + 1) * 4)
                sp.sem_inc(turn_seen, 1)
                for s in cleared:
                    sp.sem_clear(s)
                sp.sem_inc(turn_go, 1)

        @block.tensor
        def _(pe):
            def transpose_x(s, src_tile, ready, psum, tp=B_TP):
                for tc in range(TC):
                    pe.wait_ge(s[ready], tc + 1)
                    ins = nc.tensor.transpose(ps[:, tp, tc * P:(tc + 1) * P], src_tile[:, tc, :], id_sb[:])
                ins.then_inc(s[psum], 1)

            def project(s, weight, width, bank, ready, done, each=False):
                pe.wait_ge(s[ready], 1)
                for tc in range(TC):
                    dst = ps[:, bank + tc, 0:width] if each else ps[:, bank, tc * width:(tc + 1) * width]
                    ins = nc.tensor.matmul(dst, xT[:, tc * P:(tc + 1) * P], weight, start=True, stop=True)
                    if each:
                        ins.then_inc(s[done], 1)
                if not each:
                    ins.then_inc(s[done], 1)

            def dense(k):
                s = ffn[k]
                transpose_x(s, xn, "ln_ready", "xt_psum")
                project(s, weff[:], P, B_OUT, "xt_ready", "y_ready")

            def attention(a):
                s = attn[a]
                W = WINDOWS[a]
                tp_n = [0]

                def tp_fill(blocks):
                    if tp_n[0]:
                        pe.wait_ge(s["tp_read"], tp_n[0])
                    for i, t in enumerate(blocks):
                        ins = nc.tensor.transpose(ps[:, B_TP, i * P:(i + 1) * P], t, id_sb[:])
                    tp_n[0] += 1
                    ins.then_inc(s["tp_full"], 1)

                def st_unit(w, u):
                    g, j, half, n = w % NG, u // 2, u % 2, 8 * w + u
                    if u == 0 and w >= MAXED[a]:
                        pe.wait_ge(s["qm_ready"], w - MAXED[a] + 1)
                    if n >= 2:
                        pe.wait_ge(s["exp_done"], n - 1)
                    for i in range(2):
                        kc = 2 * half + i
                        ins = nc.tensor.matmul(ps[:, B_ST + 2 * (n % 2) + i, :],
                                               kpad[:, NG * j + g, kc * P:(kc + 1) * P],
                                               qT[:, g * S:(g + 1) * S], start=True, stop=True)
                    ins.then_inc(s["st_ready"], 1)

                def pv_quad(w, kc):
                    if kc == 0:
                        pe.wait_ge(s["exp_done"], 8 * (w + 1))
                        pe.wait_ge(s["v_ready"], TC)
                        if w:
                            pe.wait_ge(s["ut_copied"], w)
                    for j in range(NG):
                        ins = nc.tensor.matmul(ps[ROWS * j:ROWS * (j + 1), B_UT, :],
                                               v_sb[:, kc, NG * (w % NG) + j, :], probs[:, w % 2, j, kc, :],
                                               start=(kc == 0), stop=(kc == TC - 1))
                    if kc == TC - 1:
                        ins.then_inc(s["pv_done"], 1)

                def max_unit(g, m):
                    n, j, tc = 16 * g + m, m // TC, m % TC
                    if m == 0 and a == 0:
                        pe.wait_ge(s["qt_ready"], g + 1)
                    if n >= 2:
                        pe.wait_ge(s["sm_read"], n - 1)
                    nc.tensor.matmul(ps[:, B_SM + n % 2, :], qT[:, g * S + tc * P:g * S + (tc + 1) * P],
                                     kpad[:, NG * j + g, :], start=True, stop=True).then_inc(s["sm_ready"], 1)

                def max_rows(g):
                    pe.wait_ge(s["mx_ready"], g + 1)
                    tp_fill([mx[:, NG * tc:NG * tc + NG, :] for tc in range(TC)])

                transpose_x(s, xn, "ln_ready", "xt_psum")
                project(s, wqkv[a][:], 3 * P, 0, "xt_ready", "qkv_psum", each=True)

                def operand_bank(n, blocks):
                    if n >= 4:
                        pe.wait_ge(s["op_act"], copied(a, n - 3, 0))
                        pe.wait_ge(s["op_dve"], copied(a, n - 3, 1))
                    for i, t in enumerate(blocks):
                        ins = nc.tensor.transpose(ps[:, 4 + n % 4, i * P:(i + 1) * P], t, id_sb[:])
                    ins.then_inc(s["op_psum"], 1)

                seen = []
                for n, kind in enumerate(KINDS[a]):
                    if kind not in seen:
                        seen.append(kind)
                        if kind == "v":
                            pe.wait_ge(s["v_ready"], TC)
                            pe.wait_ge(s["one_ready"], 1)
                        else:
                            pe.wait_ge(s["lo_ready"], len(seen))
                            pe.wait_ge(s["dup_ready"], len(seen))
                    operand_bank(n, stack_block(a, n))
                banks = len(KINDS[a])
                if a == 1:
                    pe.wait_ge(s["op_act"], copied(a, banks, 0))
                    pe.wait_ge(s["op_dve"], copied(a, banks, 1))
                    for g in range(NG):
                        operand_bank(banks + g, [vT_all[:, g * S + kc * P:g * S + (kc + 1) * P] for kc in range(TC)])
                    banks += NG
                pe.wait_ge(s["op_act"], copied(a, banks, 0))
                pe.wait_ge(s["op_dve"], copied(a, banks, 1))

                if a == 1:
                    for m in range(16):
                        max_unit(0, m)
                    max_rows(0)
                for w in range(W + 2):
                    gm = w + LEAD - MAXED[a]
                    has_max = (0 if a == 0 else 1) <= gm < NG
                    for u in range(8):
                        if w < W:
                            st_unit(w, u)
                        if has_max:
                            for m in range(3 * u, min(3 * u + 3, 16)):
                                max_unit(gm, m)
                        if u % 2 and 1 <= w <= W:
                            pv_quad(w - 1, u // 2)
                        if u == 1 and w >= 2:
                            pe.wait_ge(s["ut_copied"], w - 1)
                            tp_fill([uts[w % 2][:, tc * P:(tc + 1) * P] for tc in range(TC)])
                        if a == 0 and u == 3 and 2 <= w < 2 + NG:
                            pe.wait_ge(s["state_ready"], w - 1)
                            tp_fill([stack0["q"][:, NH * tc + NG * (w - 2):NH * tc + NG * (w - 1), :]
                                     for tc in range(TC)])
                        if u == 6 and has_max:
                            max_rows(gm)
                pe.wait_ge(s["o_ready"], 1)
                for tc in range(TC):
                    ins = nc.tensor.transpose(ps[:, B_TP, tc * P:(tc + 1) * P], O[:, tc, :], id_sb[:])
                ins.then_inc(s["ot_psum"], 1)
                project(s, wo[a][:], P, B_OUT, "ot_ready", "y_ready")

            def experts(k):
                s = moe[k]
                transpose_x(s, xn, "ln_ready", "xt_psum")
                project(s, gate_sb[:], NE, B_UT, "xt_ready", "logits_ready")
                units = [(tc, ep) for tc in range(TC) for ep in range(PAIRS)]

                def gate_up(n):
                    tc, ep = units[n]
                    cols = 2 * P * (2 if ep < PAIRS - 1 else 1)
                    if n >= 2:
                        pe.wait_ge(s["h_ready"], n - 1)
                    nc.tensor.matmul(ps[:, n % 2, 0:cols], xT[:, tc * P:(tc + 1) * P],
                                     w13_sb[:, 4 * P * ep:4 * P * ep + cols],
                                     start=True, stop=True).then_inc(s["gu_ready"], 1)

                def hidden_turn(n):
                    ep = units[n][1]
                    pe.wait_ge(s["h_ready"], n + 1)
                    if n >= 2:
                        pe.wait_ge(s["ht_copied"], n - 1)
                    for i in range(2 if ep < PAIRS - 1 else 1):
                        ins = nc.tensor.transpose(ps[:, 2 + n % 2, i * P:(i + 1) * P], hb[n % 2][:, i * P:(i + 1) * P],
                                                  id_sb[:])
                    ins.then_inc(s["ht_ready"], 1)

                def down(n):
                    tc, ep = units[n]
                    pe.wait_ge(s["ht_copied"], n + 1)
                    if ep == 0 and tc >= 2:
                        pe.wait_ge(s["acc_read"], tc - 1)
                    count = 2 if ep < PAIRS - 1 else 1
                    for i in range(count):
                        e = 2 * ep + i
                        ins = nc.tensor.matmul(ps[:, 4 + tc % 2, 0:P], hT[n % 2][:, i * P:(i + 1) * P], w2_sb[:, e, :],
                                               start=(e == 0), stop=(e == NE))
                    ins.then_inc(s["mm2_done"], 1)

                for n in range(len(units) + 2):
                    if n < len(units):
                        gate_up(n)
                    if 1 <= n <= len(units):
                        hidden_turn(n - 1)
                    if n >= 2:
                        down(n - 2)

            with pe.Fori(0, NB) as b:
                dense(0)
                attention(0)
                dense(1)
                experts(0)
                attention(1)
                experts(1)
                pe.sem_inc(turn_end, 1)
                pe.wait_ge(turn_go, b + 1)

        @block.scalar
        def _(act):
            def copy_xT(s, psum="xt_psum", ready="xt_ready", affine=False):
                act.wait_ge(s[psum], 1)
                if affine:
                    nc.scalar.activation(xT[:], ps[:, B_TP, :], ACT.Identity, bias=lnb_sb[:],
                                         scale=lnw_sb[:]).then_inc(s[ready], 1)
                else:
                    nc.scalar.activation(xT[:], ps[:, B_TP, :], ACT.Copy).then_inc(s[ready], 1)

            def attention(a):
                s = attn[a]
                copy_xT(s, affine=(a == 0))
                for n, kind in enumerate(all_kinds(a)):
                    if not copies(a, n, 0):
                        continue
                    act.wait_ge(s["op_psum"], n + 1)
                    for dst, source in operand_copies(a, n, kind, 0):
                        ins = nc.scalar.activation(dst, source, ACT.Copy)
                    ins.then_inc(s["op_act"], 1)
                for w in range(WINDOWS[a]):
                    for u in range(8):
                        act.wait_ge(s["st_ready"], 8 * w + u + 1)
                        if u == 0 and w >= 2:
                            act.wait_ge(s["pv_done"], w - 1)
                        n = 8 * w + u
                        st = B_ST + 2 * (n % 2)
                        nc.scalar.activation(probs[:, w % 2, u // 2, 2 * (u % 2):2 * (u % 2) + 2, :],
                                             ps[:, st:st + 2, :], ACT.Exp).then_inc(s["exp_done"], 1)
                copy_xT(s, "ot_psum", "ot_ready")

            def experts(k):
                s = moe[k]
                copy_xT(s)
                act.wait_ge(s["shifted"], 1)
                nc.scalar.activation(el[:], el[:], ACT.Exp).then_inc(s["exped"], 1)
                act.wait_ge(s["gates_ready"], 1)
                units = [(tc, ep) for tc in range(TC) for ep in range(PAIRS)]
                for n in range(len(units) + 1):
                    if n < len(units):
                        tc, ep = units[n]
                        act.wait_ge(s["gu_ready"], n + 1)
                        if n >= 2:
                            act.wait_ge(s["h_ready"], n - 1)
                        for i in range(2 if ep < PAIRS - 1 else 1):
                            e = 2 * ep + i
                            ins = nc.scalar.activation(th[n % 2][:, i * P:(i + 1) * P], ps[:, n % 2, 2 * P * i:2 * P * i + P],
                                                       ACT.Tanh, scale=gate_half[:, tc, e:e + 1])
                        ins.then_inc(s["tanh_ready"], 1)
                    if n >= 1:
                        m = n - 1
                        cols = P * (2 if units[m][1] < PAIRS - 1 else 1)
                        act.wait_ge(s["ht_ready"], m + 1)
                        if m >= 2:
                            act.wait_ge(s["mm2_done"], m - 1)
                        nc.scalar.activation(hT[m % 2][:, 0:cols], ps[:, 2 + m % 2, 0:cols],
                                             ACT.Copy).then_inc(s["ht_copied"], 1)

            with act.Fori(0, NB) as b:
                copy_xT(ffn[0])
                attention(0)
                copy_xT(ffn[1])
                experts(0)
                attention(1)
                experts(1)
                act.sem_inc(turn_end, 1)
                act.wait_ge(turn_go, b + 1)

        @block.vector
        def _(dve):
            steps = [0]

            def link(ins):
                steps[0] += 1
                ins.then_inc(dve_step, 1)
                dve.wait_ge(dve_step, steps[0])

            def rsqrt(v, y, t):
                link(nc.vector.tensor_scalar(y.bitcast(I32), v.bitcast(I32), -0.5, RSQRT_GUESS, ALU.mult, ALU.add))
                link(nc.vector.tensor_scalar(v, v, -0.5, None, ALU.mult))
                for _ in range(3):
                    link(nc.vector.tensor_tensor(t, y, y, ALU.mult))
                    link(nc.vector.tensor_tensor(t, t, v, ALU.mult))
                    link(nc.vector.scalar_tensor_tensor(out=y, in0=t, scalar=1.5, in1=y, op0=ALU.add, op1=ALU.mult))

            def layernorm(src_tile, dst_tile, ready):
                for tc in range(TC):
                    ins = nc.vector.bn_stats(stats[:, tc, :], src_tile[:, tc, :])
                link(ins)
                for tc in range(TC):
                    ins = nc.vector.bn_aggr(mv[:, tc, :], stats[:, tc, :])
                link(ins)
                v, y, t = rs_v[:, 0:TC], rs_y[:, 0:TC], rs_t[:, 0:TC]
                link(nc.vector.tensor_scalar(v, mv[:, :, 1], EPS, None, ALU.add))
                rsqrt(v, y, t)
                for tc in range(TC):
                    nc.vector.tensor_scalar(dst_tile[:, tc, :], src_tile[:, tc, :], mv[:, tc, 0:1], y[:, tc:tc + 1],
                                            ALU.subtract, ALU.mult).then_inc(ready, 1)

            def add_output(s, base):
                dve.wait_ge(s["y_ready"], 1)
                dve.wait_ge(s[base], 1)
                link(nc.vector.tensor_tensor(X[:].rearrange("p c d -> p (c d)"), ps[:, B_OUT, :],
                                             X[:].rearrange("p c d -> p (c d)"), ALU.add))

            def dense(k):
                layernorm(X, xn, ffn[k]["ln_ready"])
                add_output(ffn[k], "xb_ready")

            def attention(a):
                s = attn[a]
                W = WINDOWS[a]
                tp_n = [0]
                bank_tp = ps[:, B_TP, :].rearrange("p (x e) -> p x e", e=ROWS)

                def tp_wait():
                    tp_n[0] += 1
                    dve.wait_ge(s["tp_full"], tp_n[0])

                if a == 0:
                    layernorm(X, R, s["x1_ready"])
                    dve.wait_ge(s["x1_ready"], TC)
                    layernorm(R, xn, s["ln_ready"])
                else:
                    layernorm(X, xn, s["ln_ready"])

                stacks = (stack0, stack1)[a]
                for tc in range(TC):
                    dve.wait_ge(s["qkv_psum"], tc + 1)
                    ins = nc.vector.tensor_tensor(qkv[:, tc, :], ps[:, tc, 0:2 * P], bqkv[a][:, 0:2 * P], ALU.add)
                    values = (v_sb[:, tc, :, 0:HD] if a == 0 else token_view(1, stacks["v"])[:, tc, :, 0:HD])
                    nc.vector.tensor_tensor(values, ps[:, tc, 2 * P:3 * P].rearrange("p (h d) -> p h d", d=HD),
                                            bqkv[a][:, 2 * P:3 * P].rearrange("p (h d) -> p h d", d=HD),
                                            ALU.add).then_inc(s["v_ready"], 1)
                dve.wait_ge(s["v_ready"], TC)
                if a == 0:
                    link(nc.vector.tensor_tensor(squares, qkv[:], qkv[:], ALU.mult))
                    link(nc.vector.tensor_reduce(rs_v[:].rearrange("p (c h) -> p c h", c=TC),
                                                 squares.rearrange("p c (h d) -> p c h d", d=HD), AX_X, ALU.add))
                    link(nc.vector.tensor_scalar(rs_v[:], rs_v[:], 1e-24, None, ALU.max))
                    rsqrt(rs_v[:], rs_y[:], rs_t[:])
                    heads = qkv[:].rearrange("p c (h d) -> p c h d", d=HD)
                    inv = rs_y[:].rearrange("p (c h) -> p c h", c=TC).unsqueeze(3).to_broadcast([P, TC, 2 * NH, HD])
                    link(nc.vector.tensor_tensor(heads, heads, inv, ALU.mult))
                for i, kind in enumerate("kq"):
                    view = token_view(a, stacks[kind])
                    off = P if kind == "k" else 0
                    source = qkv[:, :, off:off + P].rearrange("p c (h d) -> p c h d", d=HD)
                    lo = HD if kind == "k" else 2 * HD
                    nc.vector.tensor_copy(view[:, :, :, 0:HD].bitcast(F32R), source).then_inc(s["hi_ready"], 1)
                    dve.wait_ge(s["hi_ready"], i + 1)
                    nc.vector.tensor_tensor(view[:, :, :, lo:lo + HD].bitcast(F32R), source, view[:, :, :, 0:HD],
                                            ALU.subtract).then_inc(s["lo_ready"], 1)
                for n, kind in enumerate(all_kinds(a)):
                    if not copies(a, n, 1):
                        continue
                    dve.wait_ge(s["op_psum"], n + 1)
                    for dst, source in operand_copies(a, n, kind, 1):
                        ins = nc.vector.tensor_copy(dst, source)
                    ins.then_inc(s["op_dve"], 1)

                def maxima(g, units):
                    for m in units:
                        n, j, tc = 16 * g + m, m // TC, m % TC
                        dve.wait_ge(s["sm_ready"], n + 1)
                        nc.vector.tensor_reduce(negmax[:, tc, j:j + 1], ps[:, B_SM + n % 2, :], AX_X, ALU.max,
                                                negate=True).then_inc(s["sm_read"], 1)

                def max_rows_out(g):
                    dve.wait_ge(s["sm_read"], 16 * (g + 1))
                    nc.vector.tensor_copy(mx[:, :, ADD0:ROWS],
                                          negmax[:].rearrange("p c j -> p (c j)").unsqueeze(2)
                                          .to_broadcast([P, TC * NG, ROWS - ADD0])).then_inc(s["mx_ready"], 1)
                    tp_wait()
                    rows = qT[:, g * S:(g + 1) * S]
                    nc.vector.tensor_tensor(rows, ps[:, B_TP, :], rows.bitcast(F32), ALU.add).then_inc(s["qm_ready"], 1)
                    dve.wait_ge(s["qm_ready"], g + 1)
                    dve.sem_inc(s["tp_read"], 1)

                def sums_out(w):
                    dve.wait_ge(s["pv_done"], w + 1)
                    nc.vector.tensor_copy(uts[w % 2][:], ps[:, B_UT, :]).then_inc(s["ut_copied"], 1)

                if a == 1:
                    maxima(0, range(16))
                    max_rows_out(0)
                for w in range(W + 2):
                    gm = w + LEAD - MAXED[a]
                    has_max = (0 if a == 0 else 1) <= gm < NG
                    if w >= 2:
                        sums_out(w - 2)
                    if has_max:
                        maxima(gm, range(0, 6))
                    if w >= 2:
                        tp_wait()
                        link(nc.vector.reciprocal(rden[:], bank_tp[:, :, HD]))
                        inv = rden[:].unsqueeze(2).to_broadcast([P, TC * NG, HD])
                        g = (w - 2) % NG
                        if a == 0 and w - 2 < NG:
                            nc.vector.tensor_tensor(st8[:], bank_tp[:, :, 0:HD], inv, ALU.mult).then_inc(s["tp_read"], 1)
                            dve.wait_ge(s["tp_read"], tp_n[0])
                            state = st8[:].rearrange("p (c j) d -> p c j d", c=TC)
                            view = token_view(0, stack0["q"])[:, :, NG * g:NG * g + NG, :]
                            link(nc.vector.tensor_copy(view[:, :, :, 0:HD].bitcast(F32R), state))
                            nc.vector.tensor_copy(view[:, :, :, HD:2 * HD], view[:, :, :, 0:HD])
                            nc.vector.tensor_tensor(view[:, :, :, 2 * HD:3 * HD].bitcast(F32R), state,
                                                    view[:, :, :, 0:HD], ALU.subtract).then_inc(s["state_ready"], 1)
                        else:
                            heads = O[:].rearrange("p c (h d) -> p c h d", d=HD)
                            heads = heads[:, :, NG * g:NG * g + NG, :] if a == 0 else heads[:, :, g:NH:NG, :]
                            nc.vector.tensor_tensor(heads, bank_tp[:, :, 0:HD].rearrange("p (c j) d -> p c j d", c=TC),
                                                    inv.rearrange("p (c j) d -> p c j d", c=TC),
                                                    ALU.mult).then_inc(s["tp_read"], 1)
                            if g == NG - 1:
                                dve.wait_ge(s["tp_read"], tp_n[0])
                                dve.sem_inc(s["o_ready"], 1)
                    if has_max:
                        maxima(gm, range(6, 12))
                    if a == 0 and 2 <= w < 2 + NG:
                        tp_wait()
                        nc.vector.tensor_copy(qT[:, (w - 2) * S:(w - 1) * S], ps[:, B_TP, :]).then_inc(s["qt_ready"], 1)
                        dve.wait_ge(s["qt_ready"], w - 1)
                        dve.sem_inc(s["tp_read"], 1)
                    if has_max:
                        maxima(gm, range(12, 16))
                        max_rows_out(gm)
                add_output(s, "res_ready")

            def experts(k):
                s = moe[k]
                layernorm(X, xn, s["ln_ready"])
                dve.wait_ge(s["logits_ready"], 1)
                logits = ps[:, B_UT, 0:TC * NE].rearrange("p (c e) -> p c e", e=NE)
                link(nc.vector.tensor_reduce(lmax[:], logits, AX_X, ALU.max))
                nc.vector.tensor_tensor(el[:], logits, lmax[:].unsqueeze(2).to_broadcast([P, TC, NE]),
                                        ALU.subtract).then_inc(s["shifted"], 1)
                dve.wait_ge(s["exped"], 1)
                link(nc.vector.tensor_reduce(lmax[:], el[:], AX_X, ALU.add))
                link(nc.vector.reciprocal(lmax[:], lmax[:]))
                link(nc.vector.tensor_tensor(pr[:], el[:], lmax[:].unsqueeze(2).to_broadcast([P, TC, NE]), ALU.mult))
                for tc in range(TC):
                    ins = nc.vector.max(top[:, tc, :], pr[:, tc, :])
                link(ins)
                for tc in range(TC):
                    ins = nc.vector.max_index(idx[:, tc, :], top[:, tc, :], pr[:, tc, :])
                link(ins)
                link(nc.vector.tensor_copy(idxf[:], idx[:]))
                numbers = con[:, 2 * NJ:2 * NJ + NE]
                for tc in range(TC):
                    for i, dst in enumerate((first, second)):
                        ins = nc.vector.tensor_scalar(dst[:, tc, :], numbers, idxf[:, tc, i:i + 1], top[:, tc, i:i + 1],
                                                      ALU.is_equal, ALU.mult)
                link(ins)
                link(nc.vector.tensor_tensor(gate[:, :, 0:NE], first[:], second[:], ALU.add))
                link(nc.vector.tensor_scalar(gate_half[:], gate[:], 0.5, None, ALU.mult))
                link(nc.vector.tensor_tensor(gate_sq[:], gate_half[:], gate[:], ALU.mult))
                dve.sem_inc(s["gates_ready"], 1)
                units = [(tc, ep) for tc in range(TC) for ep in range(PAIRS)]

                def add_chunk(tc):
                    dve.wait_ge(s["mm2_done"], PAIRS * (tc + 1))
                    nc.vector.scalar_tensor_tensor(out=X[:, tc, :], in0=ps[:, 4 + tc % 2, 0:P], scalar=0.5,
                                                   in1=X[:, tc, :], op0=ALU.mult, op1=ALU.add).then_inc(s["acc_read"], 1)

                for n, (tc, ep) in enumerate(units):
                    count = 2 if ep < PAIRS - 1 else 1
                    gu = ps[:, n % 2, 0:2 * P * count].rearrange("p (e x) -> p e x", e=count)
                    dve.wait_ge(s["tanh_ready"], n + 1)
                    link(nc.vector.scalar_tensor_tensor(out=ga[n % 2][:, 0:P * count].rearrange("p (e x) -> p e x", e=count),
                                                        in0=th[n % 2][:, 0:P * count].rearrange("p (e x) -> p e x", e=count),
                                                        scalar=1.0, in1=gu[:, :, 0:P], op0=ALU.add, op1=ALU.mult))
                    if n >= 2:
                        dve.wait_ge(s["ht_ready"], n - 1)
                    for i in range(count):
                        e = 2 * ep + i
                        ins = nc.vector.scalar_tensor_tensor(out=hb[n % 2][:, i * P:(i + 1) * P],
                                                             in0=ga[n % 2][:, i * P:(i + 1) * P],
                                                             scalar=gate_sq[:, tc, e:e + 1], in1=gu[:, i, P:2 * P],
                                                             op0=ALU.mult, op1=ALU.mult)
                    ins.then_inc(s["h_ready"], 1)
                    if n % PAIRS == 2 and n > PAIRS:
                        add_chunk(n // PAIRS - 1)
                add_chunk(TC - 1)
                dve.wait_ge(s["acc_read"], TC)

            with dve.Fori(0, NB) as b:
                steps[0] = 0
                dve.wait_ge(x_loaded, 16)
                dense(0)
                attention(0)
                dense(1)
                experts(0)
                attention(1)
                experts(1)
                dve.sem_inc(turn_end, 1)
                dve.wait_ge(turn_go, b + 1)

        @block.gpsimd
        def _(pool):
            def wide(tile):
                return tile[:].unsqueeze(1).to_broadcast([P, TC, P])

            def dense(k):
                pool.wait_ge(ffn[k]["ln_ready"], TC)
                nc.gpsimd.tensor_tensor(X[:], X[:], wide(bffn), ALU.add).then_inc(ffn[k]["xb_ready"], 1)

            def attention(a):
                s = attn[a]
                if a == 1:
                    pool.wait_ge(s["ln_ready"], TC)
                    nc.gpsimd.memset(stack1["v"][:, :, HD:HD + 1], 1.0).then_inc(s["one_ready"], 1)
                stacks = (stack0, stack1)[a]
                for i, kind in enumerate("kq"):
                    view = stacks[kind]
                    off = 2 * HD if kind == "k" else HD
                    pool.wait_ge(s["hi_ready"], i + 1)
                    nc.gpsimd.tensor_copy(view[:, :, off:off + HD], view[:, :, 0:HD]).then_inc(s["dup_ready"], 1)
                if a == 0:
                    nc.gpsimd.tensor_tensor(X[:], X[:], R[:], ALU.add).then_inc(pool_step, 1)
                    pool.wait_ge(pool_step, 1)
                nc.gpsimd.tensor_tensor(X[:], X[:], wide(bo[a]), ALU.add).then_inc(s["res_ready"], 1)

            with pool.Fori(0, NB) as b:
                dense(0)
                attention(0)
                dense(1)
                attention(1)
                pool.sem_inc(turn_end, 1)
                pool.wait_ge(turn_go, b + 1)


def kernel(**inputs):
    import concourse.bacc as bacc
    from concourse.bass_utils import run_bass_kernel_spmd

    a = {k: np.asarray(v) for k, v in inputs.items()}

    def cat(*ws):
        return np.ascontiguousarray(np.concatenate(ws, axis=-1))

    w1 = np.concatenate([a["L1_ffn_w1"], a["L1_ffn_w1s"]], 0)
    w3 = np.concatenate([a["L1_ffn_w3"], a["L1_ffn_w3s"]], 0)
    w2 = np.concatenate([a["L1_ffn_w2"], a["L1_ffn_w2s"]], 0)
    w13 = np.stack([w1, w3], 1).transpose(2, 0, 1, 3).reshape(P, -1)

    own = (np.arange(P) % ROWS) // TOKENS_OF_BLOCK
    blocks = np.arange(NJ)
    static = (np.abs(own[:, None] - blocks) <= 1) | (blocks == 0) | (blocks == NJ - 1)
    consts = np.concatenate([static, own[:, None] == blocks, np.tile(blocks, (P, 1)), own[:, None]], 1)

    arrays = {
        "x": a["L0_attn_hidden_states"],
        "ffn_wT": a["L0_ffn_W"].T, "ffn_vT": a["L0_ffn_V_r"].T, "ffn_cT": a["L0_ffn_C"].T, "ffn_b": a["L0_ffn_b"],
        "wqkv0": cat(a["L0_attn_Wq"], a["L0_attn_Wk"], a["L0_attn_Wv"]),
        "bqkv0": cat(a["L0_attn_bq"], a["L0_attn_bk"], a["L0_attn_bv"]),
        "wo0": a["L0_attn_Wo"], "bo0": a["L0_attn_bo"],
        "lnw": a["L0_attn_ln_w"][:, None], "lnb": a["L0_attn_ln_b"][:, None],
        "wqkv1": cat(a["L1_attn_Wq"].T, a["L1_attn_Wk"].T, a["L1_attn_Wv"].T),
        "bqkv1": cat(a["L1_attn_bq"], a["L1_attn_bk"], a["L1_attn_bv"]),
        "wo1": a["L1_attn_Wo"].T, "bo1": a["L1_attn_bo"],
        "src": a["L1_attn_src_blocks"], "tgt": a["L1_attn_tgt_blocks"],
        "gateT": a["L1_ffn_gate_w"].T, "w13": w13, "w2": w2.transpose(1, 0, 2),
        "ident": np.eye(P, dtype=np.float32), "consts": consts.astype(np.float32),
    }
    arrays = {k: np.ascontiguousarray(v) for k, v in arrays.items()}
    nc = bacc.Bacc("TRN2", target_bir_lowering=False, num_devices=1)
    args = {k: nc.dram_tensor(f"in_{k}", v.shape, mybir.dt.from_np(v.dtype), kind="ExternalInput").ap()
            for k, v in arrays.items()}
    shape = arrays["x"].shape
    args["out"] = nc.dram_tensor("out_0", shape, F32, kind="ExternalOutput").ap()
    build(nc, **args)
    r = run_bass_kernel_spmd(nc, [{f"in_{k}": v for k, v in arrays.items()}], core_ids=[0])
    return r.results[0]["out_0"]
```

```python
from contextlib import ExitStack

import numpy as np

import concourse.bass as bass
from concourse import mybir

F32 = mybir.dt.float32
F32R = mybir.dt.float32r
I32 = mybir.dt.int32
U32 = mybir.dt.uint32
ALU = mybir.AluOpType
ACT = mybir.ActivationFunctionType
AX_X = mybir.AxisListType.X

P = 128
NB = 16
S = 512
TC = S // P
NH = 16
HD = P // NH
NG = 4
ROWS = 32
NE = 8
PAIRS = 5
MASK_BLOCK = 64
NJ = S // MASK_BLOCK
TOKENS_OF_BLOCK = MASK_BLOCK // NH
EPS = 1e-5
RSQRT_GUESS = float(0x5F3759DF)

B_RING = 0
RING = 4
B_UT = 4
B_TP = 5
B_SIDE = 6

ADD0 = 3 * HD


def signals(nc, ctx, prefix, names):
    return {n: ctx.enter_context(nc.semaphore(f"{prefix}_{n}")) for n in names.split()}


W_FIRST = 2 * NG
WINDOWS = 3 * NG
MAX_AT = {2: (0, 0), 3: (0, 1), 4: (0, 2), 5: (0, 3),
          7: (1, 0), 8: (1, 1), 9: (1, 2), 10: (1, 3)}
SLOTS = 16
QUADS = 3
AT_PV, AT_SUMS, AT_TURN, AT_DIVIDE, AT_STATE, AT_QUERY = 1, 2, 3, 4, 7, 8
AT_ROWS_IN, AT_ROWS, AT_ROWS_OUT = 13, 14, 15
SPLIT = 7

WEIGHTS = ((0.8, 0.5), (1.0, 0.9))


class Side:

    def __init__(self, steps):
        self.steps, self.credit = steps, 0.0

    def slot(self, weight):
        self.credit += weight
        while self.credit >= 1:
            self.credit -= 1
            next(self.steps, None)

    def finish(self):
        for _ in self.steps:
            pass


def weight(w):
    return 1.0 if w == WINDOWS else WEIGHTS[w >= SPLIT][w in MAX_AT]


FFN_SIGNALS = "ln_ready xt_psum xt_ready y_ready xb_ready y_added"
MOE_SIGNALS = ("ln_ready xt_psum xt_ready logits_ready shifted exped gates_ready gu_ready tanh_ready "
               "h_ready ht_ready ht_copied down_ready added")
PRE_SIGNALS = ("x1_ready ln_ready xt_psum xt_ready qkv_psum v_ready hi_ready extra_ready dup_ready lo_ready "
               "op_psum op_act op_dve res_ready")
OUT_SIGNALS = "ot_psum ot_ready y_ready"
WIN_SIGNALS = ("st_ready exp_done pv_done ut_copied sm_ready sm_read tp_full tp_read state_ready qt_ready "
               "mx_ready qm_ready o0_ready")


class Plan:

    def __init__(self, parts):
        self.active = [w for w in range(WINDOWS) if ("first" if w < W_FIRST else "second") in parts]
        self.maxes = [w for w in MAX_AT if ("first", "second")[MAX_AT[w][0]] in parts]
        self.ring = []
        for w in range(WINDOWS):
            for u in range(SLOTS):
                if w in self.active:
                    self.ring.append(("st", w, u))
                if w in self.maxes:
                    self.ring += [("sm", w, m) for m in max_units(u)]
        self.place = {unit: i for i, unit in enumerate(self.ring)}

    def rank(self, w):
        return sum(v < w for v in self.active)

    def max_rank(self, w):
        return sum(v < w for v in self.maxes)

    def number(self, unit):
        kind, w, i = unit
        return SLOTS * (self.rank(w) if kind == "st" else self.max_rank(w)) + i

    def bank(self, unit):
        return B_RING + self.place[unit] % RING

    def last_in_bank(self, unit):
        i = self.place[unit]
        return self.ring[i - RING] if i >= RING else None


def max_units(u):
    return range(min(16, 5 * u // 4), min(16, 5 * (u + 1) // 4))


def build(nc, x, ffn_wT, ffn_vT, ffn_cT, ffn_b, wqkv0, bqkv0, wo0, bo0, lnw, lnb,
          wqkv1, bqkv1, wo1, bo1, src, tgt, gateT, w13, w2, ident, consts, out):
    with ExitStack() as ctx:
        def sb(name, shape, dt=F32):
            return ctx.enter_context(nc.sbuf_tensor(name, shape, dt))

        ps = ctx.enter_context(nc.psum_tensor("ps", [P, 8, 512], F32))

        id_sb = sb("id_sb", [P, P])
        con = sb("con", [P, 25])
        weff = sb("weff", [P, P])
        vT = sb("vT", [ROWS, P])
        cT = sb("cT", [ROWS, P])
        wqkv = [sb(f"wqkv_{i}", [P, 3 * P]) for i in range(2)]
        bqkv = [sb(f"bqkv_{i}", [P, 3 * P]) for i in range(2)]
        wo = [sb(f"wo_{i}", [P, P]) for i in range(2)]
        bo = [sb(f"bo_{i}", [P, P]) for i in range(2)]
        bffn = sb("bffn", [P, P])
        lnw_sb = sb("lnw_sb", [P, 1])
        lnb_sb = sb("lnb_sb", [P, 1])
        gate_sb = sb("gate_sb", [P, NE])
        w13_sb = sb("w13_sb", [P, (NE + 1) * 2 * P])
        w2_sb = sb("w2_sb", [P, NE + 1, P])
        pairs_i = sb("pairs_i", [P, 2, 3], I32)
        pairs_f = sb("pairs_f", [P, 2, 3])
        hit = sb("hit", [P, 3, NJ])
        maskb = sb("maskb", [P, NJ])

        x_next = sb("x_next", [P, TC, P])
        x_a = sb("x_a", [P, TC, P])
        x_b = sb("x_b", [P, TC, P])
        x_c = sb("x_c", [P, TC, P])
        R = sb("R", [P, TC, P])
        xn = sb("xn", [P, TC, P])
        xT = sb("xT", [P, S])
        O = [sb(f"O{i}", [P, TC, P]) for i in range(2)]
        stats = sb("stats", [P, TC, 6])
        mv = sb("mv", [P, TC, 2])
        rs_v = sb("rs_v", [P, P])
        rs_y = sb("rs_y", [P, P])
        rs_t = sb("rs_t", [P, P])

        stack = sb("stack", [P, TC * NH, ROWS])
        qstack = sb("qstack", [P, TC * NG, ROWS])
        extra = sb("extra", [P, 4, NJ])
        kpad = [sb(f"kpad{i}", [P, NH, S], F32R) for i in range(2)]
        qT = [sb(f"qT{i}", [P, NG * S], F32R) for i in range(2)]
        v_sb = [sb(f"v_sb{i}", [P, TC, NH, ROWS]) for i in range(2)]
        vT_all = sb("vT_all", [P, NG * S])
        qkv = vT_all[:, 0:TC * 2 * P].rearrange("p (c x) -> p c x", c=TC)
        squares = vT_all[:, TC * 2 * P:2 * TC * 2 * P].rearrange("p (c x) -> p c x", c=TC)
        probs = sb("probs", [P, QUADS, NG, S])
        uts = sb("uts", [P, S])
        mx = sb("mx", [P, TC * NG, ROWS])
        negmax = sb("negmax", [P, TC, NG])
        rden = sb("rden", [P, TC * NG])
        st8 = sb("st8", [P, TC * NG, HD])

        th = [sb(f"th{i}", [P, 2 * P]) for i in range(2)]
        hb = [sb(f"hb{i}", [P, 2 * P]) for i in range(2)]
        hT = [sb(f"hT{i}", [P, 2 * P]) for i in range(2)]

        lmax = sb("lmax", [P, TC])
        el = sb("el", [P, TC, NE])
        pr = sb("pr", [P, TC, NE])
        top = sb("top", [P, TC, 8])
        idx = sb("idx", [P, TC, 8], U32)
        idxf = sb("idxf", [P, TC, 8])
        first = sb("first", [P, TC, NE])
        second = sb("second", [P, TC, NE])
        gate = sb("gate", [P, TC, NE + 1])
        gate_half = sb("gate_half", [P, TC, NE + 1])
        gate_sq = sb("gate_sq", [P, TC, NE + 1])

        loaded = ctx.enter_context(nc.semaphore("loaded"))
        zeroed = ctx.enter_context(nc.semaphore("zeroed"))
        prep = ctx.enter_context(nc.semaphore("prep"))
        weff_psum = ctx.enter_context(nc.semaphore("weff_psum"))
        loads = [
            (id_sb[:], ident), (con[:], consts), (weff[:], ffn_wT), (vT[:], ffn_vT), (cT[:], ffn_cT),
            (wqkv[0][:], wqkv0), (wqkv[1][:], wqkv1), (wo[0][:], wo0), (wo[1][:], wo1),
            (lnw_sb[:], lnw), (lnb_sb[:], lnb), (gate_sb[:], gateT), (w13_sb[:], w13), (w2_sb[:], w2),
            (bqkv[0][:], bqkv0.partition_broadcast(P)), (bqkv[1][:], bqkv1.partition_broadcast(P)),
            (bo[0][:], bo0.partition_broadcast(P)), (bo[1][:], bo1.partition_broadcast(P)),
            (bffn[:], ffn_b.partition_broadcast(P)),
            (pairs_i[:, 0, :], src.partition_broadcast(P)), (pairs_i[:, 1, :], tgt.partition_broadcast(P)),
        ]
        with nc.Block() as setup:
            @setup.sync
            def _(sp):
                for dst, source in loads:
                    sp.dma_start(dst, source).then_inc(loaded, 16)
                sp.wait_ge(loaded, 16 * len(loads))

            @setup.gpsimd
            def _(pool):
                zero = [extra[:], kpad[0][:].bitcast(F32), kpad[1][:].bitcast(F32), v_sb[0][:], qstack[:], mx[:],
                        gate[:], x_next[:], x_a[:], x_b[:], O[0][:], O[1][:]]
                for t in zero:
                    nc.gpsimd.memset(t, 0.0).then_inc(zeroed, 1)
                pool.wait_ge(zeroed, len(zero))
                nc.gpsimd.memset(extra[:, 0, 0:1], 1.0).then_inc(zeroed, 1)
                nc.gpsimd.memset(v_sb[0][:, :, :, HD:HD + 1], 1.0).then_inc(zeroed, 1)
                nc.gpsimd.memset(gate[:, :, NE:NE + 1], 1.0).then_inc(zeroed, 1)

            @setup.tensor
            def _(pe):
                pe.wait_ge(loaded, 16 * len(loads))
                nc.tensor.matmul(ps[:, B_SIDE, 0:P], vT[:], cT[:], start=True, stop=True).then_inc(weff_psum, 1)

            @setup.vector
            def _(dve):
                n = [0]

                def link(ins):
                    n[0] += 1
                    ins.then_inc(prep, 1)
                    dve.wait_ge(prep, n[0])

                dve.wait_ge(loaded, 16 * len(loads))
                dve.wait_ge(weff_psum, 1)
                link(nc.vector.tensor_tensor(weff[:], ps[:, B_SIDE, 0:P], weff[:], ALU.add))
                link(nc.vector.tensor_scalar(weff[:], weff[:], 0.5, None, ALU.mult))
                link(nc.vector.tensor_scalar(bffn[:], bffn[:], 0.5, None, ALU.mult))
                scale = float(HD) ** -0.5
                link(nc.vector.tensor_scalar(wqkv[1][:, 0:P], wqkv[1][:, 0:P], scale, None, ALU.mult))
                link(nc.vector.tensor_scalar(bqkv[1][:, 0:P], bqkv[1][:, 0:P], scale, None, ALU.mult))
                link(nc.vector.tensor_copy(pairs_f[:], pairs_i[:]))
                own = con[:, 3 * NJ:3 * NJ + 1]
                for r in range(3):
                    link(nc.vector.tensor_scalar(hit[:, r, :], con[:, 2 * NJ:3 * NJ], pairs_f[:, 1, r:r + 1], None,
                                                 ALU.is_equal))
                    link(nc.vector.tensor_scalar(pairs_f[:, 0, r:r + 1], pairs_f[:, 0, r:r + 1], own, None,
                                                 ALU.is_equal))
                    link(nc.vector.tensor_scalar(hit[:, r, :], hit[:, r, :], pairs_f[:, 0, r:r + 1], None, ALU.mult))
                    link(nc.vector.tensor_tensor(maskb[:], con[:, 0:NJ] if r == 0 else maskb[:], hit[:, r, :],
                                                 ALU.max))
                link(nc.vector.tensor_scalar(maskb[:], maskb[:], -1.0, 1e9, ALU.add, ALU.mult))
                dve.wait_ge(zeroed, 1)
                link(nc.vector.tensor_copy(extra[:, 2, :], con[:, NJ:2 * NJ]))
                link(nc.vector.tensor_copy(extra[:, 3, :], maskb[:]))

        pool_moved = ctx.enter_context(nc.semaphore("pool_moved"))
        turn_done = ctx.enter_context(nc.semaphore("turn_done"))
        x_loaded = ctx.enter_context(nc.semaphore("x_loaded"))
        stored = ctx.enter_context(nc.semaphore("stored"))
        dve_step = ctx.enter_context(nc.semaphore("dve_step"))
        pool_step = ctx.enter_context(nc.semaphore("pool_step"))
        ffn = [signals(nc, ctx, f"ffn{k}", FFN_SIGNALS) for k in range(2)]
        moe = [signals(nc, ctx, f"moe{k}", MOE_SIGNALS) for k in range(2)]
        pre = [signals(nc, ctx, f"pre{k}", PRE_SIGNALS) for k in range(2)]
        res = [signals(nc, ctx, f"out{k}", OUT_SIGNALS) for k in range(2)]
        win = signals(nc, ctx, "win", WIN_SIGNALS)
        turn_seen = ctx.enter_context(nc.semaphore("turn_seen"))
        turn_begun = ctx.enter_context(nc.semaphore("turn_begun"))
        turn_end = ctx.enter_context(nc.semaphore("turn_end"))
        turn_go = ctx.enter_context(nc.semaphore("turn_go"))
        cleared = [pool_moved, turn_done, x_loaded, stored, dve_step, pool_step] + [s for d in ffn + moe + pre + res + [win] for s in d.values()]

        x_dram = x.rearrange("b (c p) d -> b p c d", p=P)
        out_dram = out.rearrange("b (c p) d -> b p c d", p=P)

        KINDS = ("kq", "kqv")
        UNITS = [(tc, ep) for tc in range(TC) for ep in range(PAIRS)]

        def experts_of(ep):
            return 2 if ep < PAIRS - 1 else 1

        def bank_blocks(a, n):
            if a == 0:
                return [stack[:, tc * NH + NG * n:tc * NH + NG * n + NG, :] for tc in range(TC)]
            return [stack[:, NG * c:NG * c + NG, :] for c in range(4 * n, 4 * n + 4)]

        def token_view(a):
            if a == 0:
                return stack[:].rearrange("p (c h) e -> p c h e", c=TC)
            return stack[:].rearrange("p (h c) e -> p c h e", c=TC)

        def all_kinds(a):
            return "".join(NG * k for k in KINDS[a] + "w" * a)

        def copies(a, n, part):
            return all_kinds(a)[n] == "k" or n % 2 == part

        def copied(a, n, part):
            return sum(copies(a, i, part) for i in range(n))

        def operand_copies(a, n, part):
            kind, bank = all_kinds(a)[n], ps[:, B_SIDE + n % 2, :]
            g = n % NG
            by_four = bank.rearrange("p (c x) -> p c x", c=4)
            if kind == "k":
                pairs = []
                for j in range(2 * part, 2 * part + 2):
                    rows = slice(ROWS * j, ROWS * (j + 1))
                    if a == 0:
                        pairs.append((kpad[0][rows, NG * j + g, :], bank[rows, :]))
                    else:
                        dst = kpad[1][rows, NG * j:NG * j + NG, :].rearrange("r h (t c) -> r c (h t)", c=NH)
                        pairs.append((dst[:, 4 * g:4 * g + 4, :], by_four[rows, :, :]))
                return pairs
            if kind == "w":
                return [(v_sb[1][:, :, NG * g:NG * g + NG, :].rearrange("p c j e -> p c (j e)"), by_four)]
            if a == 0:
                return [(qT[0][:, g * S:(g + 1) * S], bank)]
            dst = (qT[1] if kind == "q" else vT_all)[:].rearrange("p (x c) -> p c x", c=NH)
            return [(dst[:, 4 * g:4 * g + 4, :], by_four)]

        FULL = frozenset(("next", "first", "second", "last"))

        def turns(eng, turn):
            turn(-1, frozenset(("next",)))
            turn(0, frozenset(("next", "first")))
            turn(1, FULL - {"last"})
            with eng.Fori(2, NB) as b:
                turn(b, FULL)
            turn(NB, frozenset(("second", "last")))
            turn(NB + 1, frozenset(("last",)))

        def run_turn(parts, slot_work, start_second, dense, experts, prelude, output):
            def before():
                if "second" in parts:
                    yield from experts(0)
                    yield from prelude(1)

            def after():
                if "last" in parts:
                    yield from output(1)
                    yield from experts(1)
                elif "first" in parts:
                    for _ in range(SLOTS + AT_DIVIDE + 1):
                        yield
                if "next" in parts:
                    yield from dense(0)
                if "first" in parts:
                    yield from output(0)
                    yield from dense(1)
                if "next" in parts:
                    yield from prelude(0)

            plan = Plan(parts)
            side = Side(before())
            for w in range(WINDOWS + 1):
                if w == SPLIT:
                    side.finish()
                    side = Side(after())
                    if "second" in parts:
                        start_second()
                for u in range(SLOTS if w < WINDOWS else AT_DIVIDE + 1):
                    slot_work(plan, w, u)
                    if plan.active:
                        side.slot(weight(w))
            side.finish()

        block = ctx.enter_context(nc.Block())

        @block.sync
        def _(sp):
            def turn(b, parts):
                if "next" in parts:
                    sp.dma_start(x_next[:], x_dram[(b + 1) % NB]).then_inc(x_loaded, 16)
                if "last" in parts:
                    sp.wait_ge(moe[1]["added"], len(UNITS))
                    sp.dma_start(out_dram[b - 2], x_c[:]).then_inc(stored, 16)
                    sp.wait_ge(stored, 16)
                sp.wait_ge(turn_end, (b + 2) * 4)
                sp.sem_inc(turn_seen, 1)
                for s in cleared:
                    sp.sem_clear(s)
                sp.sem_inc(turn_go, 1)

            turns(sp, turn)

        @block.tensor
        def _(pe):
            def turn_chunks(source, bank):
                for tc in range(TC):
                    ins = nc.tensor.transpose(ps[:, bank, tc * P:(tc + 1) * P], source[:, tc, :], id_sb[:])
                return ins

            def project(weight, width, bank):
                for tc in range(TC):
                    ins = nc.tensor.matmul(ps[:, bank, tc * width:(tc + 1) * width], xT[:, tc * P:(tc + 1) * P],
                                           weight, start=True, stop=True)
                return ins

            def dense(k):
                s = ffn[k]
                yield
                pe.wait_ge(s["ln_ready"], TC)
                turn_chunks(xn, B_SIDE).then_inc(s["xt_psum"], 1)
                yield
                pe.wait_ge(s["xt_ready"], 1)
                project(weff[:], P, B_SIDE + 1).then_inc(s["y_ready"], 1)
                yield
                yield

            def output(a):
                s = res[a]
                if a == 0:
                    pe.wait_ge(win["o0_ready"], 1)
                    pe.wait_ge(ffn[0]["y_added"], 1)
                turn_chunks(O[a], B_SIDE).then_inc(s["ot_psum"], 1)
                yield
                pe.wait_ge(s["ot_ready"], 1)
                project(wo[a][:], P, B_SIDE + 1).then_inc(s["y_ready"], 1)
                yield
                yield

            def prelude(a):
                s = pre[a]
                yield
                pe.wait_ge(s["ln_ready"], TC)
                turn_chunks(xn, B_SIDE).then_inc(s["xt_psum"], 1)
                yield
                pe.wait_ge(s["xt_ready"], 1)
                for half in range(2):
                    for tc in range(2 * half, 2 * half + 2):
                        if tc >= 2:
                            pe.wait_ge(s["v_ready"], tc - 1)
                        nc.tensor.matmul(ps[:, B_SIDE + tc % 2, 0:3 * P], xT[:, tc * P:(tc + 1) * P], wqkv[a][:],
                                         start=True, stop=True).then_inc(s["qkv_psum"], 1)
                    yield
                    yield
                if a == 0:
                    yield
                    yield
                    yield

                def fill(n, blocks):
                    if n >= 2:
                        pe.wait_ge(s["op_act"], copied(a, n - 1, 0))
                        pe.wait_ge(s["op_dve"], copied(a, n - 1, 1))
                    for i, t in enumerate(blocks):
                        ins = nc.tensor.transpose(ps[:, B_SIDE + n % 2, i * P:(i + 1) * P], t, id_sb[:])
                    ins.then_inc(s["op_psum"], 1)

                for i, kind in enumerate(KINDS[a]):
                    yield
                    if kind == "v":
                        pe.wait_ge(s["extra_ready"], i + 1)
                        pe.wait_ge(s["lo_ready"], i + 1)
                    else:
                        pe.wait_ge(s["v_ready"], TC)
                        pe.wait_ge(s["lo_ready"], i + 1)
                        pe.wait_ge(s["dup_ready"], i + 1)
                        pe.wait_ge(s["extra_ready"], i + 1)
                    for n in range(NG):
                        fill(NG * i + n, bank_blocks(a, n))
                        if n % 2:
                            yield
                if a == 1:
                    pe.wait_ge(s["op_act"], copied(a, 3 * NG, 0))
                    pe.wait_ge(s["op_dve"], copied(a, 3 * NG, 1))
                    for g in range(NG):
                        fill(3 * NG + g, [vT_all[:, g * S + kc * P:g * S + (kc + 1) * P] for kc in range(TC)])
                        if g % 2:
                            yield

            def experts(k):
                s = moe[k]
                yield
                pe.wait_ge(s["ln_ready"], TC)
                turn_chunks(xn, B_SIDE).then_inc(s["xt_psum"], 1)
                yield
                pe.wait_ge(s["xt_ready"], 1)
                project(gate_sb[:], NE, B_SIDE + 1).then_inc(s["logits_ready"], 1)
                yield
                yield
                pe.wait_ge(s["gates_ready"], 1)
                yield
                for n in range(len(UNITS) + 1):
                    if n < len(UNITS):
                        tc, ep = UNITS[n]
                        cols = 2 * P * experts_of(ep)
                        if n >= 2:
                            pe.wait_ge(s["added"], n - 1)
                        nc.tensor.matmul(ps[:, B_SIDE + n % 2, 0:cols], xT[:, tc * P:(tc + 1) * P],
                                         w13_sb[:, 4 * P * ep:4 * P * ep + cols],
                                         start=True, stop=True).then_inc(s["gu_ready"], 1)
                    if n:
                        m = n - 1
                        pe.wait_ge(s["h_ready"], m + 1)
                        for i in range(experts_of(UNITS[m][1])):
                            ins = nc.tensor.transpose(ps[:, B_SIDE + m % 2, i * P:(i + 1) * P],
                                                      hb[m % 2][:, i * P:(i + 1) * P], id_sb[:])
                        ins.then_inc(s["ht_ready"], 1)
                    yield
                    if n:
                        pe.wait_ge(s["ht_copied"], n)
                        ep = UNITS[m][1]
                        for i in range(experts_of(ep)):
                            ins = nc.tensor.matmul(ps[:, B_SIDE + m % 2, 2 * P:3 * P], hT[m % 2][:, i * P:(i + 1) * P],
                                                   w2_sb[:, 2 * ep + i, :], start=(i == 0),
                                                   stop=(i == experts_of(ep) - 1))
                        ins.then_inc(s["down_ready"], 1)
                    yield

            def tp_fill(plan, blocks):
                if tp_n[0]:
                    pe.wait_ge(win["tp_read"], tp_n[0])
                for i, t in enumerate(blocks):
                    ins = nc.tensor.transpose(ps[:, B_TP, i * P:(i + 1) * P], t, id_sb[:])
                tp_n[0] += 1
                ins.then_inc(win["tp_full"], 1)

            def ring_wait(plan, unit):
                last = plan.last_in_bank(unit)
                if last:
                    pe.wait_ge(win["exp_done" if last[0] == "st" else "sm_read"], plan.number(last) + 1)

            def values(plan, w, kc):
                a, n = int(w >= W_FIRST), TC * plan.rank(w) + kc
                pe.wait_ge(win["exp_done"], NG * (n + 1))
                if kc == 0 and plan.rank(w):
                    pe.wait_ge(win["ut_copied"], plan.rank(w))
                for j in range(NG):
                    ins = nc.tensor.matmul(ps[ROWS * j:ROWS * (j + 1), B_UT, :],
                                           v_sb[a][:, kc, NG * (w % NG) + j, :], probs[:, n % QUADS, j, :],
                                           start=(kc == 0), stop=(kc == TC - 1))
                ins.then_inc(win["pv_done"], 1)

            def slot_work(plan, w, u):
                a = int(w >= W_FIRST)
                g = w % NG
                if w in plan.active:
                    kc, j = u // NG, u % NG
                    if u == 0 and w >= NG:
                        pe.wait_ge(win["qm_ready"], sum(MAX_AT[v] <= (a, g) for v in plan.maxes))
                    ring_wait(plan, ("st", w, u))
                    nc.tensor.matmul(ps[:, plan.bank(("st", w, u)), :], kpad[a][:, NG * j + g, kc * P:(kc + 1) * P],
                                     qT[a][:, g * S:(g + 1) * S], start=True, stop=True).then_inc(win["st_ready"], 1)
                if w in plan.maxes:
                    am, gm = MAX_AT[w]
                    for m in max_units(u):
                        if m == 0 and am == 0:
                            pe.wait_ge(win["qt_ready"], gm + 1)
                        j, tc = m // TC, m % TC
                        ring_wait(plan, ("sm", w, m))
                        nc.tensor.matmul(ps[:, plan.bank(("sm", w, m)), :],
                                         qT[am][:, gm * S + tc * P:gm * S + (tc + 1) * P], kpad[am][:, NG * j + gm, :],
                                         start=True, stop=True).then_inc(win["sm_ready"], 1)
                if u % NG == AT_PV:
                    if u >= NG and w in plan.active:
                        values(plan, w, u // NG - 1)
                    elif u < NG and w - 1 in plan.active:
                        values(plan, w - 1, TC - 1)
                if u == AT_TURN and w - 1 in plan.active:
                    pe.wait_ge(win["ut_copied"], plan.rank(w))
                    tp_fill(plan, [uts[:, tc * P:(tc + 1) * P] for tc in range(TC)])
                if u == AT_STATE and w - 1 in plan.active and w - 1 < NG:
                    pe.wait_ge(win["state_ready"], w)
                    tp_fill(plan, [qstack[:, NG * tc:NG * tc + NG, :] for tc in range(TC)])
                if u == AT_ROWS and w in plan.maxes:
                    pe.wait_ge(win["mx_ready"], plan.max_rank(w) + 1)
                    tp_fill(plan, [mx[:, NG * tc:NG * tc + NG, :] for tc in range(TC)])

            def start_second():
                banks = len(all_kinds(1))
                pe.wait_ge(pre[1]["op_act"], copied(1, banks, 0))
                pe.wait_ge(pre[1]["op_dve"], copied(1, banks, 1))

            tp_n = [0]

            def turn(b, parts):
                tp_n[0] = 0
                run_turn(parts, slot_work, start_second, dense, experts, prelude, output)
                pe.drain().then_inc(turn_end, 1)
                pe.wait_ge(turn_go, b + 2)
                pe.sem_inc(turn_begun, 1)

            turns(pe, turn)

        @block.scalar
        def _(act):
            def copy_T(s, psum="xt_psum", ready="xt_ready"):
                act.wait_ge(s[psum], 1)
                nc.scalar.activation(xT[:], ps[:, B_SIDE, :], ACT.Copy).then_inc(s[ready], 1)

            def dense(k):
                yield
                copy_T(ffn[k])
                yield
                yield
                yield

            def output(a):
                copy_T(res[a], "ot_psum", "ot_ready")
                yield
                yield
                yield

            def prelude(a):
                s = pre[a]
                yield
                if a == 0:
                    act.wait_ge(s["xt_psum"], 1)
                    nc.scalar.activation(xT[:], ps[:, B_SIDE, :], ACT.Identity, bias=lnb_sb[:],
                                         scale=lnw_sb[:]).then_inc(s["xt_ready"], 1)
                else:
                    copy_T(s)
                yield
                for _ in range(4 if a == 1 else 7):
                    yield
                for n, kind in enumerate(all_kinds(a)):
                    if n % NG == 0 and kind != "w":
                        yield
                    if copies(a, n, 0):
                        act.wait_ge(s["op_psum"], n + 1)
                        for dst, source in operand_copies(a, n, 0):
                            ins = nc.scalar.activation(dst, source, ACT.Copy)
                        ins.then_inc(s["op_act"], 1)
                    if n % 2:
                        yield

            def experts(k):
                s = moe[k]
                yield
                copy_T(s)
                yield
                yield
                act.wait_ge(s["shifted"], 1)
                nc.scalar.activation(el[:], el[:], ACT.Exp).then_inc(s["exped"], 1)
                yield
                act.wait_ge(s["gates_ready"], 1)
                yield
                for n in range(len(UNITS) + 1):
                    if n < len(UNITS):
                        tc, ep = UNITS[n]
                        act.wait_ge(s["gu_ready"], n + 1)
                        for i in range(experts_of(ep)):
                            e = 2 * ep + i
                            ins = nc.scalar.activation(th[n % 2][:, i * P:(i + 1) * P],
                                                       ps[:, B_SIDE + n % 2, 2 * P * i:2 * P * i + P],
                                                       ACT.Tanh, scale=gate_half[:, tc, e:e + 1])
                        ins.then_inc(s["tanh_ready"], 1)
                    if n:
                        m = n - 1
                        cols = P * experts_of(UNITS[m][1])
                        act.wait_ge(s["ht_ready"], m + 1)
                        nc.scalar.activation(hT[m % 2][:, 0:cols], ps[:, B_SIDE + m % 2, 0:cols],
                                             ACT.Copy).then_inc(s["ht_copied"], 1)
                    yield
                    yield

            def slot_work(plan, w, u):
                if w in plan.active:
                    n = SLOTS * plan.rank(w) + u
                    quad = n // NG
                    if u % NG == 0 and quad >= QUADS:
                        act.wait_ge(win["pv_done"], quad - QUADS + 1)
                    act.wait_ge(win["st_ready"], n + 1)
                    nc.scalar.activation(probs[:, quad % QUADS, u % NG, :], ps[:, plan.bank(("st", w, u)), :],
                                         ACT.Exp).then_inc(win["exp_done"], 1)

            def turn(b, parts):
                run_turn(parts, slot_work, lambda: None, dense, experts, prelude, output)
                act.drain().then_inc(turn_end, 1)
                act.wait_ge(turn_go, b + 2)
                act.sem_inc(turn_begun, 1)

            turns(act, turn)

        @block.vector
        def _(dve):
            steps = [0]

            def link(ins):
                steps[0] += 1
                ins.then_inc(dve_step, 1)
                dve.wait_ge(dve_step, steps[0])

            def rsqrt(v, y, t):
                link(nc.vector.tensor_scalar(y.bitcast(I32), v.bitcast(I32), -0.5, RSQRT_GUESS, ALU.mult, ALU.add))
                link(nc.vector.tensor_scalar(v, v, -0.5, None, ALU.mult))
                for _ in range(3):
                    link(nc.vector.tensor_tensor(t, y, y, ALU.mult))
                    link(nc.vector.tensor_tensor(t, t, v, ALU.mult))
                    link(nc.vector.scalar_tensor_tensor(out=y, in0=t, scalar=1.5, in1=y, op0=ALU.add, op1=ALU.mult))

            def layernorm(src_tile, dst_tile, ready, v, y, t):
                for tc in range(TC):
                    ins = nc.vector.bn_stats(stats[:, tc, :], src_tile[:, tc, :])
                link(ins)
                for tc in range(TC):
                    ins = nc.vector.bn_aggr(mv[:, tc, :], stats[:, tc, :])
                link(ins)
                link(nc.vector.tensor_scalar(v, mv[:, :, 1], EPS, None, ALU.add))
                rsqrt(v, y, t)
                for tc in range(TC):
                    nc.vector.tensor_scalar(dst_tile[:, tc, :], src_tile[:, tc, :], mv[:, tc, 0:1], y[:, tc:tc + 1],
                                            ALU.subtract, ALU.mult).then_inc(ready, 1)

            rs = (rs_v[:, 0:TC], rs_y[:, 0:TC], rs_t[:, 0:TC])

            def add_output(s, X):
                dve.wait_ge(s["y_ready"], 1)
                link(nc.vector.tensor_tensor(X[:].rearrange("p c d -> p (c d)"), ps[:, B_SIDE + 1, :],
                                             X[:].rearrange("p c d -> p (c d)"), ALU.add))

            def dense(k):
                X = (x_next, x_a)[k]
                if k == 0:
                    dve.wait_ge(x_loaded, 16)
                layernorm(X, xn, ffn[k]["ln_ready"], *rs)
                yield
                yield
                yield
                dve.wait_ge(ffn[k]["xb_ready"], 1)
                add_output(ffn[k], X)
                dve.sem_inc(ffn[k]["y_added"], 1)
                yield

            def output(a):
                yield
                yield
                add_output(res[a], (x_a, x_c)[a])
                yield

            def prelude(a):
                s = pre[a]
                X = (x_next, x_b)[a]
                if a == 0:
                    layernorm(X, R, s["x1_ready"], *rs)
                    dve.wait_ge(s["x1_ready"], TC)
                    layernorm(R, xn, s["ln_ready"], *rs)
                else:
                    layernorm(X, xn, s["ln_ready"], *rs)
                yield
                yield
                for half in range(2):
                    yield
                    for tc in range(2 * half, 2 * half + 2):
                        bank = ps[:, B_SIDE + tc % 2, :]
                        dve.wait_ge(s["qkv_psum"], tc + 1)
                        nc.vector.tensor_tensor(qkv[:, tc, :], bank[:, 0:2 * P], bqkv[a][:, 0:2 * P], ALU.add)
                        dst = v_sb[0][:, tc, :, 0:HD] if a == 0 else \
                            squares[:, tc, 0:P].rearrange("p (h d) -> p h d", d=HD)
                        nc.vector.tensor_tensor(dst, bank[:, 2 * P:3 * P].rearrange("p (h d) -> p h d", d=HD),
                                                bqkv[a][:, 2 * P:3 * P].rearrange("p (h d) -> p h d", d=HD),
                                                ALU.add).then_inc(s["v_ready"], 1)
                    yield
                dve.wait_ge(s["v_ready"], TC)
                if a == 0:
                    link(nc.vector.tensor_tensor(squares, qkv, qkv, ALU.mult))
                    link(nc.vector.tensor_reduce(rs_v[:].rearrange("p (c h) -> p c h", c=TC),
                                                 squares.rearrange("p c (h d) -> p c h d", d=HD), AX_X, ALU.add))
                    yield
                    link(nc.vector.tensor_scalar(rs_v[:], rs_v[:], 1e-24, None, ALU.max))
                    rsqrt(rs_v[:], rs_y[:], rs_t[:])
                    yield
                    heads = qkv.rearrange("p c (h d) -> p c h d", d=HD)
                    inv = rs_y[:].rearrange("p (c h) -> p c h", c=TC).unsqueeze(3).to_broadcast([P, TC, 2 * NH, HD])
                    link(nc.vector.tensor_tensor(heads, heads, inv, ALU.mult))
                    yield
                view = token_view(a)
                for n, kind in enumerate(all_kinds(a)):
                    i = n // NG
                    if n % NG == 0 and kind != "w":
                        if i:
                            dve.wait_ge(s["op_psum"], NG * i)
                        if kind == "v":
                            nc.vector.tensor_copy(view[:, :, :, 0:HD], squares[:, :, 0:P].rearrange(
                                "p c (h d) -> p c h d", d=HD)).then_inc(s["lo_ready"], 1)
                        else:
                            off = P if kind == "k" else 0
                            source = qkv[:, :, off:off + P].rearrange("p c (h d) -> p c h d", d=HD)
                            lo = HD if kind == "k" else 2 * HD
                            nc.vector.tensor_copy(view[:, :, :, 0:HD].bitcast(F32R), source).then_inc(s["hi_ready"], 1)
                            dve.wait_ge(s["hi_ready"], i + 1)
                            nc.vector.tensor_tensor(view[:, :, :, lo:lo + HD].bitcast(F32R), source,
                                                    view[:, :, :, 0:HD], ALU.subtract).then_inc(s["lo_ready"], 1)
                        yield
                    if copies(a, n, 1):
                        dve.wait_ge(s["op_psum"], n + 1)
                        if kind == "v":
                            dve.wait_ge(s["lo_ready"], i + 1)
                        for dst, source in operand_copies(a, n, 1):
                            ins = nc.vector.tensor_copy(dst, source)
                        ins.then_inc(s["op_dve"], 1)
                    if n % 2:
                        yield

            def experts(k):
                s = moe[k]
                X = (x_b, x_c)[k]
                layernorm(X, xn, s["ln_ready"], *rs)
                yield
                yield
                yield
                dve.wait_ge(s["logits_ready"], 1)
                logits = ps[:, B_SIDE + 1, 0:TC * NE].rearrange("p (c e) -> p c e", e=NE)
                link(nc.vector.tensor_reduce(lmax[:], logits, AX_X, ALU.max))
                nc.vector.tensor_tensor(el[:], logits, lmax[:].unsqueeze(2).to_broadcast([P, TC, NE]),
                                        ALU.subtract).then_inc(s["shifted"], 1)
                yield
                dve.wait_ge(s["exped"], 1)
                link(nc.vector.tensor_reduce(lmax[:], el[:], AX_X, ALU.add))
                link(nc.vector.reciprocal(lmax[:], lmax[:]))
                link(nc.vector.tensor_tensor(pr[:], el[:], lmax[:].unsqueeze(2).to_broadcast([P, TC, NE]), ALU.mult))
                for tc in range(TC):
                    ins = nc.vector.max(top[:, tc, :], pr[:, tc, :])
                link(ins)
                for tc in range(TC):
                    ins = nc.vector.max_index(idx[:, tc, :], top[:, tc, :], pr[:, tc, :])
                link(ins)
                link(nc.vector.tensor_copy(idxf[:], idx[:]))
                numbers = con[:, 2 * NJ:2 * NJ + NE]
                for tc in range(TC):
                    for i, dst in enumerate((first, second)):
                        ins = nc.vector.tensor_scalar(dst[:, tc, :], numbers, idxf[:, tc, i:i + 1], top[:, tc, i:i + 1],
                                                      ALU.is_equal, ALU.mult)
                link(ins)
                link(nc.vector.tensor_tensor(gate[:, :, 0:NE], first[:], second[:], ALU.add))
                link(nc.vector.tensor_scalar(gate_half[:], gate[:], 0.5, None, ALU.mult))
                nc.vector.tensor_tensor(gate_sq[:], gate_half[:], gate[:], ALU.mult).then_inc(s["gates_ready"], 1)
                dve.wait_ge(s["gates_ready"], 1)
                yield
                for n in range(len(UNITS) + 1):
                    yield
                    if n < len(UNITS):
                        tc, ep = UNITS[n]
                        count = experts_of(ep)
                        gu = ps[:, B_SIDE + n % 2, 0:2 * P * count].rearrange("p (e x) -> p e x", e=count)
                        dve.wait_ge(s["tanh_ready"], n + 1)
                        link(nc.vector.scalar_tensor_tensor(
                            out=th[n % 2][:, 0:P * count].rearrange("p (e x) -> p e x", e=count),
                            in0=th[n % 2][:, 0:P * count].rearrange("p (e x) -> p e x", e=count),
                            scalar=1.0, in1=gu[:, :, 0:P], op0=ALU.add, op1=ALU.mult))
                        for i in range(count):
                            e = 2 * ep + i
                            ins = nc.vector.scalar_tensor_tensor(out=hb[n % 2][:, i * P:(i + 1) * P],
                                                                 in0=th[n % 2][:, i * P:(i + 1) * P],
                                                                 scalar=gate_sq[:, tc, e:e + 1], in1=gu[:, i, P:2 * P],
                                                                 op0=ALU.mult, op1=ALU.mult)
                        ins.then_inc(s["h_ready"], 1)
                    if n:
                        tc = UNITS[n - 1][0]
                        dve.wait_ge(s["down_ready"], n)
                        dve.wait_ge(s["added"], n - 1) if n > 1 else None
                        nc.vector.scalar_tensor_tensor(out=X[:, tc, :], in0=ps[:, B_SIDE + (n - 1) % 2, 2 * P:3 * P],
                                                       scalar=0.5, in1=X[:, tc, :], op0=ALU.mult,
                                                       op1=ALU.add).then_inc(s["added"], 1)
                    if n == len(UNITS):
                        dve.wait_ge(s["added"], n)
                    yield

            bank_tp = ps[:, B_TP, :].rearrange("p (x e) -> p x e", e=ROWS)
            tp_n = [0]

            def tp_wait():
                tp_n[0] += 1
                dve.wait_ge(win["tp_full"], tp_n[0])

            def divide(w):
                g = w % NG
                tp_wait()
                link(nc.vector.reciprocal(rden[:], bank_tp[:, :, HD]))
                inv = rden[:].unsqueeze(2).to_broadcast([P, TC * NG, HD])
                if w < NG:
                    nc.vector.tensor_tensor(st8[:], bank_tp[:, :, 0:HD], inv, ALU.mult).then_inc(win["tp_read"], 1)
                    dve.wait_ge(win["tp_read"], tp_n[0])
                    link(nc.vector.tensor_copy(qstack[:, :, 0:HD].bitcast(F32R), st8[:]))
                    nc.vector.tensor_copy(qstack[:, :, HD:2 * HD], qstack[:, :, 0:HD])
                    nc.vector.tensor_tensor(qstack[:, :, 2 * HD:3 * HD].bitcast(F32R), st8[:], qstack[:, :, 0:HD],
                                            ALU.subtract).then_inc(win["state_ready"], 1)
                    return
                a = int(w >= W_FIRST)
                heads = O[a][:].rearrange("p c (h d) -> p c h d", d=HD)
                heads = heads[:, :, NG * g:NG * g + NG, :] if a == 0 else heads[:, :, g:NH:NG, :]
                nc.vector.tensor_tensor(heads, bank_tp[:, :, 0:HD].rearrange("p (c j) d -> p c j d", c=TC),
                                        inv.rearrange("p (c j) d -> p c j d", c=TC),
                                        ALU.mult).then_inc(win["tp_read"], 1)
                if w == W_FIRST - 1:
                    dve.wait_ge(win["tp_read"], tp_n[0])
                    dve.sem_inc(win["o0_ready"], 1)

            def slot_work(plan, w, u):
                if w in plan.maxes:
                    a, g = MAX_AT[w]
                    for m in max_units(u):
                        j, tc = m // TC, m % TC
                        unit = ("sm", w, m)
                        dve.wait_ge(win["sm_ready"], plan.number(unit) + 1)
                        nc.vector.tensor_reduce(negmax[:, tc, j:j + 1], ps[:, plan.bank(unit), :], AX_X, ALU.max,
                                                negate=True).then_inc(win["sm_read"], 1)
                if u == AT_SUMS and w - 1 in plan.active:
                    dve.wait_ge(win["pv_done"], TC * plan.rank(w))
                    nc.vector.tensor_copy(uts[:], ps[:, B_UT, :]).then_inc(win["ut_copied"], 1)
                if u == AT_DIVIDE and w - 1 in plan.active:
                    divide(w - 1)
                if u == AT_QUERY and w - 1 in plan.active and w - 1 < NG:
                    tp_wait()
                    nc.vector.tensor_copy(qT[0][:, (w - 1) * S:w * S], ps[:, B_TP, :]).then_inc(win["qt_ready"], 1)
                    dve.wait_ge(win["qt_ready"], w)
                    dve.sem_inc(win["tp_read"], 1)
                if u == AT_ROWS_IN and w in plan.maxes:
                    dve.wait_ge(win["sm_read"], SLOTS * (plan.max_rank(w) + 1))
                    nc.vector.tensor_copy(mx[:, :, ADD0:ROWS],
                                          negmax[:].rearrange("p c j -> p (c j)").unsqueeze(2)
                                          .to_broadcast([P, TC * NG, ROWS - ADD0])).then_inc(win["mx_ready"], 1)
                if u == AT_ROWS_OUT and w in plan.maxes:
                    a, g = MAX_AT[w]
                    tp_wait()
                    rows = qT[a][:, g * S:(g + 1) * S]
                    nc.vector.tensor_tensor(rows, ps[:, B_TP, :], rows.bitcast(F32), ALU.add).then_inc(win["qm_ready"], 1)
                    dve.wait_ge(win["qm_ready"], plan.max_rank(w) + 1)
                    dve.sem_inc(win["tp_read"], 1)

            def start_second():
                dve.wait_ge(pre[1]["op_act"], copied(1, len(all_kinds(1)), 0))

            def turn(b, parts):
                steps[0] = tp_n[0] = 0
                run_turn(parts, slot_work, start_second, dense, experts, prelude, output)
                dve.sem_inc(turn_done, 1)
                dve.drain().then_inc(turn_end, 1)
                dve.wait_ge(turn_go, b + 2)
                dve.sem_inc(turn_begun, 1)

            turns(dve, turn)

        @block.gpsimd
        def _(pool):
            def wide(tile):
                return tile[:].unsqueeze(1).to_broadcast([P, TC, P])

            def dense(k):
                yield
                X = (x_next, x_a)[k]
                pool.wait_ge(ffn[k]["ln_ready"], TC)
                nc.gpsimd.tensor_tensor(X[:], X[:], wide(bffn), ALU.add).then_inc(ffn[k]["xb_ready"], 1)
                yield
                yield
                yield

            def output(a):
                yield
                yield
                yield

            def experts(k):
                for _ in range(5 + 2 * (len(UNITS) + 1)):
                    yield

            def prelude(a):
                s = pre[a]
                X = (x_next, x_b)[a]
                yield
                if a == 0:
                    pool.wait_ge(s["x1_ready"], TC)
                    nc.gpsimd.tensor_tensor(X[:], X[:], R[:], ALU.add).then_inc(pool_step, 1)
                    pool.wait_ge(pool_step, 1)
                else:
                    pool.wait_ge(s["ln_ready"], TC)
                nc.gpsimd.tensor_tensor(X[:], X[:], wide(bo[a]), ALU.add).then_inc(s["res_ready"], 1)
                yield
                for _ in range(4 if a == 1 else 7):
                    yield
                for i, kind in enumerate(KINDS[a]):
                    if i:
                        pool.wait_ge(s["op_psum"], NG * i)
                    if kind == "v":
                        nc.gpsimd.memset(stack[:, :, HD:HD + 1], 1.0).then_inc(s["extra_ready"], 1)
                    else:
                        columns = extra[:, 2 * a + i, :].unsqueeze(1).to_broadcast([P, TC * NH, NJ])
                        nc.gpsimd.tensor_copy(stack[:, :, ADD0:ROWS], columns).then_inc(s["extra_ready"], 1)
                        off = 2 * HD if kind == "k" else HD
                        pool.wait_ge(s["hi_ready"], i + 1)
                        nc.gpsimd.tensor_copy(stack[:, :, off:off + HD], stack[:, :, 0:HD]).then_inc(s["dup_ready"], 1)
                    yield
                    yield
                    yield
                if a == 1:
                    yield
                    yield

            def turn(b, parts):
                run_turn(parts, lambda plan, w, u: None, lambda: None, dense, experts, prelude, output)
                pool.wait_ge(turn_done, 1)
                if "last" in parts:
                    pool.wait_ge(stored, 16)
                moved = 0
                for dst, source in ((x_c, x_b), (x_b, x_a), (x_a, x_next)):
                    nc.gpsimd.tensor_copy(dst[:], source[:]).then_inc(pool_moved, 1)
                    moved += 1
                    pool.wait_ge(pool_moved, moved)
                pool.drain().then_inc(turn_end, 1)
                pool.wait_ge(turn_go, b + 2)
                pool.sem_inc(turn_begun, 1)

            turns(pool, turn)


def kernel(**inputs):
    import concourse.bacc as bacc
    from concourse.bass_utils import run_bass_kernel_spmd

    a = {k: np.asarray(v) for k, v in inputs.items()}

    def cat(*ws):
        return np.ascontiguousarray(np.concatenate(ws, axis=-1))

    w1 = np.concatenate([a["L1_ffn_w1"], a["L1_ffn_w1s"]], 0)
    w3 = np.concatenate([a["L1_ffn_w3"], a["L1_ffn_w3s"]], 0)
    w2 = np.concatenate([a["L1_ffn_w2"], a["L1_ffn_w2s"]], 0)
    w13 = np.stack([w1, w3], 1).transpose(2, 0, 1, 3).reshape(P, -1)

    own = (np.arange(P) % ROWS) // TOKENS_OF_BLOCK
    blocks = np.arange(NJ)
    static = (np.abs(own[:, None] - blocks) <= 1) | (blocks == 0) | (blocks == NJ - 1)
    consts = np.concatenate([static, own[:, None] == blocks, np.tile(blocks, (P, 1)), own[:, None]], 1)

    arrays = {
        "x": a["L0_attn_hidden_states"],
        "ffn_wT": a["L0_ffn_W"].T, "ffn_vT": a["L0_ffn_V_r"].T, "ffn_cT": a["L0_ffn_C"].T, "ffn_b": a["L0_ffn_b"],
        "wqkv0": cat(a["L0_attn_Wq"], a["L0_attn_Wk"], a["L0_attn_Wv"]),
        "bqkv0": cat(a["L0_attn_bq"], a["L0_attn_bk"], a["L0_attn_bv"]),
        "wo0": a["L0_attn_Wo"], "bo0": a["L0_attn_bo"],
        "lnw": a["L0_attn_ln_w"][:, None], "lnb": a["L0_attn_ln_b"][:, None],
        "wqkv1": cat(a["L1_attn_Wq"].T, a["L1_attn_Wk"].T, a["L1_attn_Wv"].T),
        "bqkv1": cat(a["L1_attn_bq"], a["L1_attn_bk"], a["L1_attn_bv"]),
        "wo1": a["L1_attn_Wo"].T, "bo1": a["L1_attn_bo"],
        "src": a["L1_attn_src_blocks"], "tgt": a["L1_attn_tgt_blocks"],
        "gateT": a["L1_ffn_gate_w"].T, "w13": w13, "w2": w2.transpose(1, 0, 2),
        "ident": np.eye(P, dtype=np.float32), "consts": consts.astype(np.float32),
    }
    arrays = {k: np.ascontiguousarray(v) for k, v in arrays.items()}
    nc = bacc.Bacc("TRN2", target_bir_lowering=False, num_devices=1)
    args = {k: nc.dram_tensor(f"in_{k}", v.shape, mybir.dt.from_np(v.dtype), kind="ExternalInput").ap()
            for k, v in arrays.items()}
    shape = arrays["x"].shape
    args["out"] = nc.dram_tensor("out_0", shape, F32, kind="ExternalOutput").ap()
    build(nc, **args)
    r = run_bass_kernel_spmd(nc, [{f"in_{k}": v for k, v in arrays.items()}], core_ids=[0])
    return r.results[0]["out_0"]
```

```python
from contextlib import ExitStack

import numpy as np

import concourse.bass as bass
from concourse import mybir

F32 = mybir.dt.float32
F32R = mybir.dt.float32r
I32 = mybir.dt.int32
U32 = mybir.dt.uint32
ALU = mybir.AluOpType
ACT = mybir.ActivationFunctionType
AX_X = mybir.AxisListType.X

P = 128
NB = 16
S = 512
TC = S // P
NH = 16
HD = P // NH
NG = 4
ROWS = 32
NE = 8
PAIRS = 5
MASK_BLOCK = 64
NJ = S // MASK_BLOCK
TOKENS_OF_BLOCK = MASK_BLOCK // NH
EPS = 1e-5
RSQRT_GUESS = float(0x5F3759DF)

B_RING = 0
RING = 3
B_THIRD = 3
B_UT = 4
B_TP = 5
B_SIDE = 6

ADD0 = 3 * HD


def signals(nc, ctx, prefix, names):
    return {n: ctx.enter_context(nc.semaphore(f"{prefix}_{n}")) for n in names.split()}


W_FIRST = 2 * NG
WINDOWS = 3 * NG
MAX_AT = {2: (0, 0), 3: (0, 1), 4: (0, 2), 5: (0, 3),
          6: (1, 0), 7: (1, 1), 8: (1, 2), 9: (1, 3)}
SLOTS = 16
QUADS = 3
AT_PV, AT_SUMS, AT_TURN, AT_DIVIDE, AT_STATE, AT_QUERY = 1, 2, 4, 5, 7, 8
AT_ROWS_IN, AT_ROWS, AT_ROWS_OUT = 0, 11, 13
SPLIT = 6

LN_STEPS = 4
INV_STEPS = 6
GATE_STEPS = 5
STACK_STEPS = 2


class Side:

    def __init__(self, steps):
        self.steps, self.reached = steps, set()

    def step(self):
        mark = next(self.steps, DONE)
        if mark:
            self.reached.add(mark)

    def slot(self, held):
        if not (held and HOLD in self.reached):
            self.step()

    def run_to(self, mark):
        while not {mark, DONE} & self.reached:
            self.step()


SECOND_MADE, HOLD, DONE = "second made", "hold", "done"


def idle(n):
    for _ in range(n):
        yield


FFN_SIGNALS = "ln_ready xt_psum xt_ready y_ready xb_ready y_added"
MOE_SIGNALS = ("ln_ready xt_psum xt_ready xt_hi_ready xt_split logits_ready shifted exped gates_ready gu_ready "
               "tanh_ready h_ready ht_ready ht_copied down_ready added")
PRE_SIGNALS = ("x1_ready ln_ready xt_psum xt_ready qkv_psum v_ready hi_ready extra_ready dup_ready lo_ready "
               "op_psum op_act op_dve res_ready")
OUT_SIGNALS = "ot_psum ot_ready y_ready"
WIN_SIGNALS = ("st_ready exp_done pv_done ut_copied sm_ready sm_read tp_full tp_read state_ready qt_ready "
               "mx_ready qm_ready o0_ready")


class Plan:

    def __init__(self, parts):
        self.active = [w for w in range(WINDOWS) if ("first" if w < W_FIRST else "second") in parts]
        self.maxes = [w for w in MAX_AT if ("first", "second")[MAX_AT[w][0]] in parts]
        self.ring = []
        for w in range(WINDOWS):
            for u in range(SLOTS):
                if w in self.active:
                    self.ring.append(("st", w, u))
                if w in self.maxes:
                    self.ring.append(("sm", w, u))
        self.place = {unit: i for i, unit in enumerate(self.ring)}

    def rank(self, w):
        return sum(v < w for v in self.active)

    def max_rank(self, w):
        return sum(v < w for v in self.maxes)

    def number(self, unit):
        kind, w, i = unit
        return SLOTS * (self.rank(w) if kind == "st" else self.max_rank(w)) + i

    def bank(self, unit):
        return B_RING + self.place[unit] % RING

    def last_in_bank(self, unit):
        i = self.place[unit]
        return self.ring[i - RING] if i >= RING else None


def build(nc, x, ffn_wT, ffn_vT, ffn_cT, ffn_b, wqkv0, bqkv0, wo0, bo0, lnw, lnb,
          wqkv1, bqkv1, wo1, bo1, src, tgt, gateT, w13, w2, ident, consts, out):
    with ExitStack() as ctx:
        def sb(name, shape, dt=F32):
            return ctx.enter_context(nc.sbuf_tensor(name, shape, dt))

        ps = ctx.enter_context(nc.psum_tensor("ps", [P, 8, 512], F32))

        id_sb = sb("id_sb", [P, P])
        con = sb("con", [P, 25])
        weff = sb("weff", [P, P])
        vT = sb("vT", [ROWS, P])
        cT = sb("cT", [ROWS, P])
        wqkv = [sb(f"wqkv_{i}", [P, 3 * P]) for i in range(2)]
        bqkv = [sb(f"bqkv_{i}", [P, 3 * P]) for i in range(2)]
        wo = [sb(f"wo_{i}", [P, P]) for i in range(2)]
        bo = [sb(f"bo_{i}", [P, P]) for i in range(2)]
        bffn = sb("bffn", [P, P])
        lnw_sb = sb("lnw_sb", [P, 1])
        lnb_sb = sb("lnb_sb", [P, 1])
        gate_sb = sb("gate_sb", [P, NE])
        w13_hi = sb("w13_hi", [P, (NE + 1) * 2 * P], F32R)
        w13_lo = sb("w13_lo", [P, (NE + 1) * 2 * P], F32R)
        xT_hi = sb("xT_hi", [P, S], F32R)
        xT_lo = sb("xT_lo", [P, S], F32R)
        w2_sb = sb("w2_sb", [P, NE + 1, P])
        pairs_i = sb("pairs_i", [P, 2, 3], I32)
        pairs_f = sb("pairs_f", [P, 2, 3])
        hit = sb("hit", [P, 3, NJ])
        maskb = sb("maskb", [P, NJ])

        x_next = sb("x_next", [P, TC, P])
        x_a = sb("x_a", [P, TC, P])
        x_b = sb("x_b", [P, TC, P])
        x_c = sb("x_c", [P, TC, P])
        R = sb("R", [P, TC, P])
        xn = sb("xn", [P, TC, P])
        xT = sb("xT", [P, S])
        O = [sb(f"O{i}", [P, TC, P]) for i in range(2)]
        stats = sb("stats", [P, TC, 6])
        mv = sb("mv", [P, TC, 2])
        early_stats = sb("early_stats", [P, TC, 6])
        early_mv = sb("early_mv", [P, TC, 2])
        early_rs = sb("early_rs", [P, 3, TC])
        rs_v = sb("rs_v", [P, P])
        rs_y = sb("rs_y", [P, P])
        rs_t = sb("rs_t", [P, P])

        stack = sb("stack", [P, TC * NH, ROWS])
        qstack = sb("qstack", [P, TC * NG, ROWS])
        extra = sb("extra", [P, 4, NJ])
        kpad = [sb(f"kpad{i}", [P, NH, S], F32R) for i in range(2)]
        qT = [sb(f"qT{i}", [P, NG * S], F32R) for i in range(2)]
        v_sb = [sb(f"v_sb{i}", [P, TC, NH, ROWS]) for i in range(2)]
        vT_all = sb("vT_all", [P, NG * S])
        qkv = vT_all[:, 0:TC * 2 * P].rearrange("p (c x) -> p c x", c=TC)
        squares = vT_all[:, TC * 2 * P:2 * TC * 2 * P].rearrange("p (c x) -> p c x", c=TC)
        probs = sb("probs", [P, QUADS, NG, S])
        uts = sb("uts", [P, S])
        mx = sb("mx", [P, TC * NG, ROWS])
        negmax = sb("negmax", [P, TC, NG])
        rden = sb("rden", [P, TC * NG])
        st8 = sb("st8", [P, TC * NG, HD])

        th = [sb(f"th{i}", [P, 2 * P]) for i in range(2)]
        hb = [sb(f"hb{i}", [P, 2 * P]) for i in range(2)]
        hT = [sb(f"hT{i}", [P, 2 * P]) for i in range(2)]

        lmax = sb("lmax", [P, TC])
        el = sb("el", [P, TC, NE])
        pr = sb("pr", [P, TC, NE])
        top = sb("top", [P, TC, 8])
        idx = sb("idx", [P, TC, 8], U32)
        idxf = sb("idxf", [P, TC, 8])
        first = sb("first", [P, TC, NE])
        second = sb("second", [P, TC, NE])
        gate = sb("gate", [P, TC, NE + 1])
        gate_half = sb("gate_half", [P, TC, NE + 1])
        gate_sq = sb("gate_sq", [P, TC, NE + 1])

        loaded = ctx.enter_context(nc.semaphore("loaded"))
        zeroed = ctx.enter_context(nc.semaphore("zeroed"))
        prep = ctx.enter_context(nc.semaphore("prep"))
        weff_psum = ctx.enter_context(nc.semaphore("weff_psum"))
        w13_sb = probs[:].rearrange("p q j s -> p (q j s)")[:, 0:(NE + 1) * 2 * P]
        loads = [
            (id_sb[:], ident), (con[:], consts), (weff[:], ffn_wT), (vT[:], ffn_vT), (cT[:], ffn_cT),
            (wqkv[0][:], wqkv0), (wqkv[1][:], wqkv1), (wo[0][:], wo0), (wo[1][:], wo1),
            (lnw_sb[:], lnw), (lnb_sb[:], lnb), (gate_sb[:], gateT), (w13_sb, w13), (w2_sb[:], w2),
            (bqkv[0][:], bqkv0.partition_broadcast(P)), (bqkv[1][:], bqkv1.partition_broadcast(P)),
            (bo[0][:], bo0.partition_broadcast(P)), (bo[1][:], bo1.partition_broadcast(P)),
            (bffn[:], ffn_b.partition_broadcast(P)),
            (pairs_i[:, 0, :], src.partition_broadcast(P)), (pairs_i[:, 1, :], tgt.partition_broadcast(P)),
        ]
        with nc.Block() as setup:
            @setup.sync
            def _(sp):
                for dst, source in loads:
                    sp.dma_start(dst, source).then_inc(loaded, 16)
                sp.wait_ge(loaded, 16 * len(loads))

            @setup.gpsimd
            def _(pool):
                zero = [extra[:], kpad[0][:].bitcast(F32), kpad[1][:].bitcast(F32), v_sb[0][:], qstack[:], mx[:],
                        gate[:], x_next[:], x_a[:], x_b[:], O[0][:], O[1][:]]
                for t in zero:
                    nc.gpsimd.memset(t, 0.0).then_inc(zeroed, 1)
                pool.wait_ge(zeroed, len(zero))
                nc.gpsimd.memset(extra[:, 0, 0:1], 1.0).then_inc(zeroed, 1)
                nc.gpsimd.memset(v_sb[0][:, :, :, HD:HD + 1], 1.0).then_inc(zeroed, 1)
                nc.gpsimd.memset(gate[:, :, NE:NE + 1], 1.0).then_inc(zeroed, 1)

            @setup.tensor
            def _(pe):
                pe.wait_ge(loaded, 16 * len(loads))
                nc.tensor.matmul(ps[:, B_SIDE, 0:P], vT[:], cT[:], start=True, stop=True).then_inc(weff_psum, 1)

            @setup.vector
            def _(dve):
                n = [0]

                def link(ins):
                    n[0] += 1
                    ins.then_inc(prep, 1)
                    dve.wait_ge(prep, n[0])

                dve.wait_ge(loaded, 16 * len(loads))
                dve.wait_ge(weff_psum, 1)
                link(nc.vector.tensor_tensor(weff[:], ps[:, B_SIDE, 0:P], weff[:], ALU.add))
                link(nc.vector.tensor_copy(w13_hi[:], w13_sb))
                link(nc.vector.tensor_tensor(w13_lo[:], w13_sb, w13_hi[:].bitcast(F32), ALU.subtract))
                link(nc.vector.tensor_scalar(weff[:], weff[:], 0.5, None, ALU.mult))
                link(nc.vector.tensor_scalar(bffn[:], bffn[:], 0.5, None, ALU.mult))
                scale = float(HD) ** -0.5
                link(nc.vector.tensor_scalar(wqkv[1][:, 0:P], wqkv[1][:, 0:P], scale, None, ALU.mult))
                link(nc.vector.tensor_scalar(bqkv[1][:, 0:P], bqkv[1][:, 0:P], scale, None, ALU.mult))
                link(nc.vector.tensor_copy(pairs_f[:], pairs_i[:]))
                own = con[:, 3 * NJ:3 * NJ + 1]
                for r in range(3):
                    link(nc.vector.tensor_scalar(hit[:, r, :], con[:, 2 * NJ:3 * NJ], pairs_f[:, 1, r:r + 1], None,
                                                 ALU.is_equal))
                    link(nc.vector.tensor_scalar(pairs_f[:, 0, r:r + 1], pairs_f[:, 0, r:r + 1], own, None,
                                                 ALU.is_equal))
                    link(nc.vector.tensor_scalar(hit[:, r, :], hit[:, r, :], pairs_f[:, 0, r:r + 1], None, ALU.mult))
                    link(nc.vector.tensor_tensor(maskb[:], con[:, 0:NJ] if r == 0 else maskb[:], hit[:, r, :],
                                                 ALU.max))
                link(nc.vector.tensor_scalar(maskb[:], maskb[:], -1.0, 1e9, ALU.add, ALU.mult))
                dve.wait_ge(zeroed, 1)
                link(nc.vector.tensor_copy(extra[:, 2, :], con[:, NJ:2 * NJ]))
                link(nc.vector.tensor_copy(extra[:, 3, :], maskb[:]))

        moved = ctx.enter_context(nc.semaphore("moved"))
        x_loaded = ctx.enter_context(nc.semaphore("x_loaded"))
        stored = ctx.enter_context(nc.semaphore("stored"))
        dve_step = ctx.enter_context(nc.semaphore("dve_step"))
        pool_step = ctx.enter_context(nc.semaphore("pool_step"))
        ffn = [signals(nc, ctx, f"ffn{k}", FFN_SIGNALS) for k in range(2)]
        moe = [signals(nc, ctx, f"moe{k}", MOE_SIGNALS) for k in range(2)]
        pre = [signals(nc, ctx, f"pre{k}", PRE_SIGNALS) for k in range(2)]
        res = [signals(nc, ctx, f"out{k}", OUT_SIGNALS) for k in range(2)]
        win = signals(nc, ctx, "win", WIN_SIGNALS)
        turn_seen = ctx.enter_context(nc.semaphore("turn_seen"))
        turn_begun = ctx.enter_context(nc.semaphore("turn_begun"))
        turn_end = ctx.enter_context(nc.semaphore("turn_end"))
        turn_go = ctx.enter_context(nc.semaphore("turn_go"))
        cleared = [moved, x_loaded, stored, dve_step, pool_step]
        cleared += [s for d in ffn + moe + pre + res + [win] for s in d.values()]

        x_dram = x.rearrange("b (c p) d -> b p c d", p=P)
        out_dram = out.rearrange("b (c p) d -> b p c d", p=P)

        KINDS = ("kq", "kqv")
        UNITS = [(tc, ep) for tc in range(TC) for ep in range(PAIRS)]

        def experts_of(ep):
            return 2 if ep < PAIRS - 1 else 1

        def unit_bank(n):
            return ps[:, (B_SIDE, B_SIDE + 1, B_THIRD)[n % 3], :]

        def bank_blocks(a, n):
            if a == 0:
                return [stack[:, tc * NH + NG * n:tc * NH + NG * n + NG, :] for tc in range(TC)]
            return [stack[:, NG * c:NG * c + NG, :] for c in range(4 * n, 4 * n + 4)]

        def token_view(a):
            if a == 0:
                return stack[:].rearrange("p (c h) e -> p c h e", c=TC)
            return stack[:].rearrange("p (h c) e -> p c h e", c=TC)

        def all_kinds(a):
            return "".join(NG * k for k in KINDS[a] + "w" * a)

        def copies(a, n, part):
            return all_kinds(a)[n] == "k" or n % 2 == part

        def copied(a, n, part):
            return sum(copies(a, i, part) for i in range(n))

        def operand_copies(a, n, part):
            kind, bank = all_kinds(a)[n], ps[:, B_SIDE + n % 2, :]
            g = n % NG
            by_four = bank.rearrange("p (c x) -> p c x", c=4)
            if kind == "k":
                pairs = []
                for j in range(2 * part, 2 * part + 2):
                    rows = slice(ROWS * j, ROWS * (j + 1))
                    if a == 0:
                        pairs.append((kpad[0][rows, NG * j + g, :], bank[rows, :]))
                    else:
                        dst = kpad[1][rows, NG * j:NG * j + NG, :].rearrange("r h (t c) -> r c (h t)", c=NH)
                        pairs.append((dst[:, 4 * g:4 * g + 4, :], by_four[rows, :, :]))
                return pairs
            if kind == "w":
                return [(v_sb[1][:, :, NG * g:NG * g + NG, :].rearrange("p c j e -> p c (j e)"), by_four)]
            if a == 0:
                return [(qT[0][:, g * S:(g + 1) * S], bank)]
            dst = (qT[1] if kind == "q" else vT_all)[:].rearrange("p (x c) -> p c x", c=NH)
            return [(dst[:, 4 * g:4 * g + 4, :], by_four)]

        FULL = frozenset(("next", "first", "second", "last"))

        def turns(eng, turn):
            turn(-1, frozenset(("next",)))
            turn(0, frozenset(("next", "first")))
            turn(1, FULL - {"last"})
            with eng.Fori(2, NB) as b:
                turn(b, FULL)
            turn(NB, frozenset(("second", "last")))
            turn(NB + 1, frozenset(("last",)))

        def run_turn(parts, slot_work, start_second, dense, experts, prelude, output):
            def steps():
                if "second" in parts:
                    yield from experts(0, False)
                    yield from prelude(1, False)
                    yield SECOND_MADE
                if "last" in parts:
                    yield from output(1, False)
                    yield from experts(1, "next" in parts)
                if "next" in parts:
                    yield from dense(0, "last" in parts)
                if "first" in parts:
                    yield HOLD
                    yield from output(0, "next" in parts)
                    yield from dense(1, False)
                if "next" in parts:
                    yield from prelude(0, "first" in parts)

            plan = Plan(parts)
            side = Side(steps())
            for w in range(WINDOWS + 1):
                if w == SPLIT and "second" in parts:
                    side.run_to(SECOND_MADE)
                    start_second()
                for u in range(SLOTS if w < WINDOWS else AT_DIVIDE + 1):
                    slot_work(plan, w, u)
                    if plan.active:
                        side.slot((w, u) <= (W_FIRST, AT_DIVIDE))
            side.run_to(DONE)

        block = ctx.enter_context(nc.Block())

        @block.sync
        def _(sp):
            def turn(b, parts):
                if "next" in parts:
                    sp.dma_start(x_next[:], x_dram[(b + 1) % NB]).then_inc(x_loaded, 16)
                if "last" in parts:
                    sp.wait_ge(moe[1]["added"], len(UNITS))
                    sp.dma_start(out_dram[b - 2], x_c[:]).then_inc(stored, 16)
                    sp.wait_ge(stored, 16)
                sp.wait_ge(turn_end, (b + 2) * 4)
                sp.sem_inc(turn_seen, 1)
                for s in cleared:
                    sp.sem_clear(s)
                sp.sem_inc(turn_go, 1)

            turns(sp, turn)

        @block.tensor
        def _(pe):
            def turn_chunks(source, bank):
                for tc in range(TC):
                    ins = nc.tensor.transpose(ps[:, bank, tc * P:(tc + 1) * P], source[:, tc, :], id_sb[:])
                return ins

            def project(weight, width, bank):
                for tc in range(TC):
                    ins = nc.tensor.matmul(ps[:, bank, tc * width:(tc + 1) * width], xT[:, tc * P:(tc + 1) * P],
                                           weight, start=True, stop=True)
                return ins

            def dense(k, early):
                s = ffn[k]
                if early:
                    pe.wait_ge(moe[1]["added"], len(UNITS))
                else:
                    yield from idle(LN_STEPS)
                pe.wait_ge(s["ln_ready"], TC)
                turn_chunks(R if k == 0 else xn, B_SIDE).then_inc(s["xt_psum"], 1)
                yield
                pe.wait_ge(s["xt_ready"], 1)
                project(weff[:], P, B_SIDE + 1).then_inc(s["y_ready"], 1)
                yield
                yield

            def output(a, early):
                s = res[a]
                if a == 0:
                    pe.wait_ge(win["o0_ready"], 1)
                    pe.wait_ge(ffn[0]["y_added"], 1)
                turn_chunks(O[a], B_SIDE).then_inc(s["ot_psum"], 1)
                yield
                pe.wait_ge(s["ot_ready"], 1)
                project(wo[a][:], P, B_SIDE + 1).then_inc(s["y_ready"], 1)
                yield
                yield

            def prelude(a, early):
                s = pre[a]
                yield from idle((1 if a else 0 if early else 2) * LN_STEPS)
                pe.wait_ge(s["ln_ready"], TC)
                turn_chunks(xn, B_SIDE).then_inc(s["xt_psum"], 1)
                yield
                pe.wait_ge(s["xt_ready"], 1)
                for tc in range(TC):
                    if early and tc == 1:
                        pe.wait_ge(ffn[1]["y_added"], 1)
                    if tc >= 2:
                        pe.wait_ge(s["v_ready"], tc - 1)
                    nc.tensor.matmul(ps[:, B_SIDE + tc % 2, 0:3 * P], xT[:, tc * P:(tc + 1) * P], wqkv[a][:],
                                     start=True, stop=True).then_inc(s["qkv_psum"], 1)
                    yield
                yield
                if a == 0:
                    yield from idle(INV_STEPS)

                def fill(n, blocks):
                    if n >= 2:
                        pe.wait_ge(s["op_act"], copied(a, n - 1, 0))
                        pe.wait_ge(s["op_dve"], copied(a, n - 1, 1))
                    for i, t in enumerate(blocks):
                        ins = nc.tensor.transpose(ps[:, B_SIDE + n % 2, i * P:(i + 1) * P], t, id_sb[:])
                    ins.then_inc(s["op_psum"], 1)

                for i, kind in enumerate(KINDS[a]):
                    yield from idle(STACK_STEPS)
                    if kind == "v":
                        pe.wait_ge(s["extra_ready"], i + 1)
                        pe.wait_ge(s["lo_ready"], i + 1)
                    else:
                        pe.wait_ge(s["v_ready"], TC)
                        pe.wait_ge(s["lo_ready"], i + 1)
                        pe.wait_ge(s["dup_ready"], i + 1)
                        pe.wait_ge(s["extra_ready"], i + 1)
                    for n in range(NG):
                        fill(NG * i + n, bank_blocks(a, n))
                        yield
                    yield
                if a == 1:
                    pe.wait_ge(s["op_act"], copied(a, 3 * NG, 0))
                    pe.wait_ge(s["op_dve"], copied(a, 3 * NG, 1))
                    for g in range(NG):
                        fill(3 * NG + g, [vT_all[:, g * S + kc * P:g * S + (kc + 1) * P] for kc in range(TC)])
                        yield
                    yield
                    pe.wait_ge(s["op_act"], copied(1, 4 * NG, 0))
                    pe.wait_ge(s["op_dve"], copied(1, 4 * NG, 1))

            def experts(k, early):
                s = moe[k]
                yield from idle(LN_STEPS)
                pe.wait_ge(s["ln_ready"], TC)
                turn_chunks(xn, B_SIDE).then_inc(s["xt_psum"], 1)
                yield
                pe.wait_ge(s["xt_ready"], 1)
                project(gate_sb[:], NE, B_SIDE + 1).then_inc(s["logits_ready"], 1)
                yield from idle(2 + GATE_STEPS)
                pe.wait_ge(s["gates_ready"], 1)
                pe.wait_ge(s["xt_split"], 1)
                yield
                for n in range(len(UNITS) + 2):
                    if n >= 2:
                        m = n - 2
                        pe.wait_ge(s["ht_copied"], m + 1)
                        ep = UNITS[m][1]
                        for i in range(experts_of(ep)):
                            ins = nc.tensor.matmul(unit_bank(m)[:, 2 * P:3 * P], hT[m % 2][:, i * P:(i + 1) * P],
                                                   w2_sb[:, 2 * ep + i, :], start=(i == 0),
                                                   stop=(i == experts_of(ep) - 1))
                        ins.then_inc(s["down_ready"], 1)
                    if n < len(UNITS):
                        tc, ep = UNITS[n]
                        cols = 2 * P * experts_of(ep)
                        if n >= 3:
                            pe.wait_ge(s["added"], n - 2)
                        hi, lo = (t[:, tc * P:(tc + 1) * P] for t in (xT_hi, xT_lo))
                        w_hi, w_lo = (t[:, 4 * P * ep:4 * P * ep + cols] for t in (w13_hi, w13_lo))
                        nc.tensor.matmul(unit_bank(n)[:, 0:cols], hi, w_hi, start=True, stop=False)
                        nc.tensor.matmul(unit_bank(n)[:, 0:cols], hi, w_lo, start=False, stop=False)
                        nc.tensor.matmul(unit_bank(n)[:, 0:cols], lo, w_hi,
                                         start=False, stop=True).then_inc(s["gu_ready"], 1)
                    yield
                    if 1 <= n <= len(UNITS):
                        m = n - 1
                        pe.wait_ge(s["h_ready"], m + 1)
                        for i in range(experts_of(UNITS[m][1])):
                            ins = nc.tensor.transpose(unit_bank(m)[:, i * P:(i + 1) * P],
                                                      hb[m % 2][:, i * P:(i + 1) * P], id_sb[:])
                        ins.then_inc(s["ht_ready"], 1)
                    yield

            def tp_fill(plan, blocks):
                if tp_n[0]:
                    pe.wait_ge(win["tp_read"], tp_n[0])
                for i, t in enumerate(blocks):
                    ins = nc.tensor.transpose(ps[:, B_TP, i * P:(i + 1) * P], t, id_sb[:])
                tp_n[0] += 1
                ins.then_inc(win["tp_full"], 1)

            def ring_wait(plan, unit):
                last = plan.last_in_bank(unit)
                if last:
                    pe.wait_ge(win["exp_done" if last[0] == "st" else "sm_read"], plan.number(last) + 1)

            def values(plan, w, kc):
                a, n = int(w >= W_FIRST), TC * plan.rank(w) + kc
                pe.wait_ge(win["exp_done"], NG * (n + 1))
                if kc == 0 and plan.rank(w):
                    pe.wait_ge(win["ut_copied"], plan.rank(w))
                for j in range(NG):
                    ins = nc.tensor.matmul(ps[ROWS * j:ROWS * (j + 1), B_UT, :],
                                           v_sb[a][:, kc, NG * (w % NG) + j, :], probs[:, n % QUADS, j, :],
                                           start=(kc == 0), stop=(kc == TC - 1))
                ins.then_inc(win["pv_done"], 1)

            def slot_work(plan, w, u):
                a = int(w >= W_FIRST)
                g = w % NG
                if w in plan.active:
                    kc, j = u // NG, u % NG
                    if u == 0 and w >= NG:
                        pe.wait_ge(win["qm_ready"], sum(MAX_AT[v] <= (a, g) for v in plan.maxes))
                    ring_wait(plan, ("st", w, u))
                    nc.tensor.matmul(ps[:, plan.bank(("st", w, u)), :], kpad[a][:, NG * j + g, kc * P:(kc + 1) * P],
                                     qT[a][:, g * S:(g + 1) * S], start=True, stop=True).then_inc(win["st_ready"], 1)
                if w in plan.maxes:
                    am, gm = MAX_AT[w]
                    if u == 0 and am == 0:
                        pe.wait_ge(win["qt_ready"], gm + 1)
                    j, tc = u // TC, u % TC
                    ring_wait(plan, ("sm", w, u))
                    nc.tensor.matmul(ps[:, plan.bank(("sm", w, u)), :],
                                     qT[am][:, gm * S + tc * P:gm * S + (tc + 1) * P], kpad[am][:, NG * j + gm, :],
                                     start=True, stop=True).then_inc(win["sm_ready"], 1)
                if u % NG == AT_PV:
                    if u >= NG and w in plan.active:
                        values(plan, w, u // NG - 1)
                    elif u < NG and w - 1 in plan.active:
                        values(plan, w - 1, TC - 1)
                if u == AT_TURN and w - 1 in plan.active:
                    pe.wait_ge(win["ut_copied"], plan.rank(w))
                    tp_fill(plan, [uts[:, tc * P:(tc + 1) * P] for tc in range(TC)])
                if u == AT_STATE and w - 1 in plan.active and w - 1 < NG:
                    pe.wait_ge(win["state_ready"], w)
                    tp_fill(plan, [qstack[:, NG * tc:NG * tc + NG, :] for tc in range(TC)])
                if u == AT_ROWS and w - 1 in plan.maxes:
                    pe.wait_ge(win["mx_ready"], plan.max_rank(w))
                    tp_fill(plan, [mx[:, NG * tc:NG * tc + NG, :] for tc in range(TC)])

            tp_n = [0]

            def turn(b, parts):
                tp_n[0] = 0
                run_turn(parts, slot_work, lambda: None, dense, experts, prelude, output)
                pe.drain().then_inc(turn_end, 1)
                pe.wait_ge(turn_go, b + 2)
                pe.sem_inc(turn_begun, 1)

            turns(pe, turn)

        @block.scalar
        def _(act):
            def copy_T(s, psum="xt_psum", ready="xt_ready"):
                act.wait_ge(s[psum], 1)
                nc.scalar.activation(xT[:], ps[:, B_SIDE, :], ACT.Copy).then_inc(s[ready], 1)

            def move(dst, source):
                moves[0] += 1
                nc.scalar.activation(dst[:], source[:], ACT.Copy).then_inc(moved, 1)
                act.wait_ge(moved, moves[0])

            def move_to_last():
                if "last" in now[0]:
                    act.wait_ge(stored, 16)
                act.wait_ge(pre[1]["res_ready"], 1)
                move(x_c, x_b)

            def dense(k, early):
                yield from idle(0 if early else LN_STEPS)
                copy_T(ffn[k])
                yield
                yield
                yield

            def output(a, early):
                if a == 0 and "second" in now[0]:
                    move_to_last()
                copy_T(res[a], "ot_psum", "ot_ready")
                yield
                yield
                yield

            def prelude(a, early):
                s = pre[a]
                yield from idle((1 if a else 0 if early else 2) * LN_STEPS)
                if a == 0:
                    act.wait_ge(s["xt_psum"], 1)
                    nc.scalar.activation(xT[:], ps[:, B_SIDE, :], ACT.Identity, bias=lnb_sb[:],
                                         scale=lnw_sb[:]).then_inc(s["xt_ready"], 1)
                else:
                    copy_T(s)
                yield
                yield from idle(5 if a else 5 + INV_STEPS)
                if a == 0:
                    if "first" in now[0]:
                        act.wait_ge(ffn[1]["y_added"], 1)
                        move(x_b, x_a)
                    act.wait_ge(s["res_ready"], 1)
                    move(x_a, x_next)
                for n, kind in enumerate(all_kinds(a)):
                    if n % NG == 0 and kind != "w":
                        yield from idle(STACK_STEPS)
                    if n % NG == 0:
                        yield
                    if copies(a, n, 0):
                        act.wait_ge(s["op_psum"], n + 1)
                        for dst, source in operand_copies(a, n, 0):
                            ins = nc.scalar.activation(dst, source, ACT.Copy)
                        ins.then_inc(s["op_act"], 1)
                    yield

            def experts(k, early):
                s = moe[k]
                yield from idle(LN_STEPS)
                copy_T(s)
                yield from idle(3)
                act.wait_ge(s["shifted"], 1)
                nc.scalar.activation(el[:], el[:], ACT.Exp).then_inc(s["exped"], 1)
                yield from idle(GATE_STEPS)
                act.wait_ge(s["gates_ready"], 1)
                yield
                for n in range(len(UNITS) + 2):
                    if n < len(UNITS):
                        tc, ep = UNITS[n]
                        act.wait_ge(s["gu_ready"], n + 1)
                        for i in range(experts_of(ep)):
                            e = 2 * ep + i
                            ins = nc.scalar.activation(th[n % 2][:, i * P:(i + 1) * P],
                                                       unit_bank(n)[:, 2 * P * i:2 * P * i + P],
                                                       ACT.Tanh, scale=gate_half[:, tc, e:e + 1])
                        ins.then_inc(s["tanh_ready"], 1)
                    yield
                    if 1 <= n <= len(UNITS):
                        m = n - 1
                        cols = P * experts_of(UNITS[m][1])
                        act.wait_ge(s["ht_ready"], m + 1)
                        nc.scalar.activation(hT[m % 2][:, 0:cols], unit_bank(m)[:, 0:cols],
                                             ACT.Copy).then_inc(s["ht_copied"], 1)
                    yield

            def slot_work(plan, w, u):
                if w in plan.active:
                    n = SLOTS * plan.rank(w) + u
                    quad = n // NG
                    if u % NG == 0 and quad >= QUADS:
                        act.wait_ge(win["pv_done"], quad - QUADS + 1)
                    act.wait_ge(win["st_ready"], n + 1)
                    nc.scalar.activation(probs[:, quad % QUADS, u % NG, :], ps[:, plan.bank(("st", w, u)), :],
                                         ACT.Exp).then_inc(win["exp_done"], 1)

            moves, now = [0], [None]

            def turn(b, parts):
                moves[0], now[0] = 0, parts
                run_turn(parts, slot_work, lambda: None, dense, experts, prelude, output)
                if "second" in parts and "first" not in parts:
                    move_to_last()
                act.drain().then_inc(turn_end, 1)
                act.wait_ge(turn_go, b + 2)
                act.sem_inc(turn_begun, 1)

            turns(act, turn)

        @block.vector
        def _(dve):
            steps = [0]

            def link(ins):
                steps[0] += 1
                ins.then_inc(dve_step, 1)
                dve.wait_ge(dve_step, steps[0])

            def rsqrt(v, y, t):
                link(nc.vector.tensor_scalar(y.bitcast(I32), v.bitcast(I32), -0.5, RSQRT_GUESS, ALU.mult, ALU.add))
                for i in range(3):
                    if i:
                        yield
                    link(nc.vector.scalar_tensor_tensor(out=t, in0=y, scalar=-0.5, in1=y, op0=ALU.mult,
                                                        op1=ALU.mult))
                    link(nc.vector.tensor_tensor(t, t, v, ALU.mult))
                    link(nc.vector.scalar_tensor_tensor(out=y, in0=t, scalar=1.5, in1=y, op0=ALU.add, op1=ALU.mult))

            def layernorm(src_tile, dst_tile, ready, stats, mv, v, y, t):
                for tc in range(TC):
                    ins = nc.vector.bn_stats(stats[:, tc, :], src_tile[:, tc, :])
                link(ins)
                for tc in range(TC):
                    ins = nc.vector.bn_aggr(mv[:, tc, :], stats[:, tc, :])
                link(ins)
                link(nc.vector.tensor_scalar(v, mv[:, :, 1], EPS, None, ALU.add))
                yield
                yield from rsqrt(v, y, t)
                for tc in range(TC):
                    nc.vector.tensor_scalar(dst_tile[:, tc, :], src_tile[:, tc, :], mv[:, tc, 0:1], y[:, tc:tc + 1],
                                            ALU.subtract, ALU.mult).then_inc(ready, 1)
                yield

            rs = (stats, mv, rs_v[:, 0:TC], rs_y[:, 0:TC], rs_t[:, 0:TC])
            rs_early = (early_stats, early_mv, early_rs[:, 0, :], early_rs[:, 1, :], early_rs[:, 2, :])
            along = [iter(())]

            def norms_first(scratch):
                yield from layernorm(x_next, R, pre[0]["x1_ready"], *scratch)
                dve.wait_ge(pre[0]["x1_ready"], TC)
                yield from layernorm(R, xn, pre[0]["ln_ready"], *scratch)

            def norm_next():
                dve.wait_ge(x_loaded, 16)
                yield from layernorm(x_next, R, ffn[0]["ln_ready"], *rs_early)

            def add_output(s, X):
                dve.wait_ge(s["y_ready"], 1)
                link(nc.vector.tensor_tensor(X[:].rearrange("p c d -> p (c d)"), ps[:, B_SIDE + 1, :],
                                             X[:].rearrange("p c d -> p (c d)"), ALU.add))

            def dense(k, early):
                X = (x_next, x_a)[k]
                if k == 1:
                    for _ in layernorm(X, xn, ffn[1]["ln_ready"], *rs):
                        next(along[0], None)
                        yield
                elif not early:
                    yield from norm_next()
                yield
                if k == 1:
                    dve.wait_ge(ffn[1]["xt_psum"], 1)
                    next(along[0], None)
                yield
                dve.wait_ge(ffn[k]["xb_ready"], 1)
                add_output(ffn[k], X)
                dve.sem_inc(ffn[k]["y_added"], 1)
                yield

            def output(a, early):
                if early:
                    along[0] = norms_first(rs_early)
                    next(along[0])
                yield
                if early:
                    next(along[0])
                yield
                add_output(res[a], (x_a, x_c)[a])
                if early:
                    next(along[0])
                yield

            def prelude(a, early):
                s = pre[a]
                X = (x_next, x_b)[a]
                if a == 0:
                    if not early:
                        yield from norms_first(rs)
                else:
                    yield from layernorm(X, xn, s["ln_ready"], *rs)
                yield
                yield
                for tc in range(TC):
                    bank = ps[:, B_SIDE + tc % 2, :]
                    dve.wait_ge(s["qkv_psum"], tc + 1)
                    nc.vector.tensor_tensor(qkv[:, tc, :], bank[:, 0:2 * P], bqkv[a][:, 0:2 * P], ALU.add)
                    dst = v_sb[0][:, tc, :, 0:HD] if a == 0 else \
                        squares[:, tc, 0:P].rearrange("p (h d) -> p h d", d=HD)
                    nc.vector.tensor_tensor(dst, bank[:, 2 * P:3 * P].rearrange("p (h d) -> p h d", d=HD),
                                            bqkv[a][:, 2 * P:3 * P].rearrange("p (h d) -> p h d", d=HD),
                                            ALU.add).then_inc(s["v_ready"], 1)
                    yield
                dve.wait_ge(s["v_ready"], TC)
                if a == 0:
                    link(nc.vector.tensor_tensor(squares, qkv, qkv, ALU.mult))
                    link(nc.vector.tensor_reduce(rs_v[:].rearrange("p (c h) -> p c h", c=TC),
                                                 squares.rearrange("p c (h d) -> p c h d", d=HD), AX_X, ALU.add))
                    yield
                    link(nc.vector.tensor_scalar(rs_v[:], rs_v[:], 1e-24, None, ALU.max))
                    yield from rsqrt(rs_v[:], rs_y[:], rs_t[:])
                    yield
                    heads = qkv.rearrange("p c (h d) -> p c h d", d=HD)
                    inv = rs_y[:].rearrange("p (c h) -> p c h", c=TC).unsqueeze(3).to_broadcast([P, TC, 2 * NH, HD])
                    link(nc.vector.tensor_tensor(heads, heads, inv, ALU.mult))
                    yield
                    yield
                view = token_view(a)
                for n, kind in enumerate(all_kinds(a)):
                    i = n // NG
                    if n % NG == 0 and kind != "w":
                        if i:
                            dve.wait_ge(s["op_psum"], NG * i)
                        if kind == "v":
                            nc.vector.tensor_copy(view[:, :, :, 0:HD], squares[:, :, 0:P].rearrange(
                                "p c (h d) -> p c h d", d=HD)).then_inc(s["lo_ready"], 1)
                        else:
                            off = P if kind == "k" else 0
                            source = qkv[:, :, off:off + P].rearrange("p c (h d) -> p c h d", d=HD)
                            lo = HD if kind == "k" else 2 * HD
                            nc.vector.tensor_copy(view[:, :, :, 0:HD].bitcast(F32R), source).then_inc(s["hi_ready"], 1)
                            dve.wait_ge(s["hi_ready"], i + 1)
                            nc.vector.tensor_tensor(view[:, :, :, lo:lo + HD].bitcast(F32R), source,
                                                    view[:, :, :, 0:HD], ALU.subtract).then_inc(s["lo_ready"], 1)
                        yield from idle(STACK_STEPS)
                    if n % NG == 0:
                        yield
                    if copies(a, n, 1):
                        dve.wait_ge(s["op_psum"], n + 1)
                        for dst, source in operand_copies(a, n, 1):
                            ins = nc.vector.tensor_copy(dst, source)
                        ins.then_inc(s["op_dve"], 1)
                    yield

            def experts(k, early):
                s = moe[k]
                X = (x_b, x_c)[k]
                yield from layernorm(X, xn, s["ln_ready"], *rs)
                yield
                dve.wait_ge(s["xt_ready"], 1)
                nc.vector.tensor_copy(xT_hi[:], xT[:]).then_inc(s["xt_hi_ready"], 1)
                yield
                dve.wait_ge(s["logits_ready"], 1)
                logits = ps[:, B_SIDE + 1, 0:TC * NE].rearrange("p (c e) -> p c e", e=NE)
                link(nc.vector.tensor_reduce(lmax[:], logits, AX_X, ALU.max))
                nc.vector.tensor_tensor(el[:], logits, lmax[:].unsqueeze(2).to_broadcast([P, TC, NE]),
                                        ALU.subtract).then_inc(s["shifted"], 1)
                yield
                dve.wait_ge(s["xt_hi_ready"], 1)
                nc.vector.tensor_tensor(xT_lo[:], xT[:], xT_hi[:].bitcast(F32), ALU.subtract).then_inc(s["xt_split"], 1)
                yield
                dve.wait_ge(s["exped"], 1)
                link(nc.vector.tensor_reduce(lmax[:], el[:], AX_X, ALU.add))
                link(nc.vector.reciprocal(lmax[:], lmax[:]))
                link(nc.vector.tensor_tensor(pr[:], el[:], lmax[:].unsqueeze(2).to_broadcast([P, TC, NE]), ALU.mult))
                yield
                for tc in range(TC):
                    ins = nc.vector.max(top[:, tc, :], pr[:, tc, :])
                link(ins)
                yield
                for tc in range(TC):
                    ins = nc.vector.max_index(idx[:, tc, :], top[:, tc, :], pr[:, tc, :])
                link(ins)
                link(nc.vector.tensor_copy(idxf[:], idx[:]))
                yield
                numbers = con[:, 2 * NJ:2 * NJ + NE]
                for tc in range(TC):
                    for i, dst in enumerate((first, second)):
                        ins = nc.vector.tensor_scalar(dst[:, tc, :], numbers, idxf[:, tc, i:i + 1], top[:, tc, i:i + 1],
                                                      ALU.is_equal, ALU.mult)
                link(ins)
                yield
                link(nc.vector.tensor_tensor(gate[:, :, 0:NE], first[:], second[:], ALU.add))
                link(nc.vector.tensor_scalar(gate_half[:], gate[:], 0.5, None, ALU.mult))
                nc.vector.tensor_tensor(gate_sq[:], gate_half[:], gate[:], ALU.mult).then_inc(s["gates_ready"], 1)
                dve.wait_ge(s["gates_ready"], 1)
                yield
                along[0] = norm_next() if early else iter(())
                for n in range(len(UNITS) + 2):
                    if n < LN_STEPS:
                        next(along[0], None)
                    yield
                    if n >= 2:
                        m = n - 2
                        tc = UNITS[m][0]
                        dve.wait_ge(s["down_ready"], m + 1)
                        if m:
                            dve.wait_ge(s["added"], m)
                        nc.vector.scalar_tensor_tensor(out=X[:, tc, :], in0=unit_bank(m)[:, 2 * P:3 * P], scalar=0.5,
                                                       in1=X[:, tc, :], op0=ALU.mult,
                                                       op1=ALU.add).then_inc(s["added"], 1)
                    if n < len(UNITS):
                        tc, ep = UNITS[n]
                        count = experts_of(ep)
                        gu = unit_bank(n)[:, 0:2 * P * count].rearrange("p (e x) -> p e x", e=count)
                        dve.wait_ge(s["tanh_ready"], n + 1)
                        link(nc.vector.scalar_tensor_tensor(
                            out=th[n % 2][:, 0:P * count].rearrange("p (e x) -> p e x", e=count),
                            in0=th[n % 2][:, 0:P * count].rearrange("p (e x) -> p e x", e=count),
                            scalar=1.0, in1=gu[:, :, 0:P], op0=ALU.add, op1=ALU.mult))
                        for i in range(count):
                            e = 2 * ep + i
                            ins = nc.vector.scalar_tensor_tensor(out=hb[n % 2][:, i * P:(i + 1) * P],
                                                                 in0=th[n % 2][:, i * P:(i + 1) * P],
                                                                 scalar=gate_sq[:, tc, e:e + 1], in1=gu[:, i, P:2 * P],
                                                                 op0=ALU.mult, op1=ALU.mult)
                        ins.then_inc(s["h_ready"], 1)
                    if n == len(UNITS) + 1:
                        dve.wait_ge(s["added"], len(UNITS))
                    yield

            bank_tp = ps[:, B_TP, :].rearrange("p (x e) -> p x e", e=ROWS)
            tp_n = [0]

            def tp_wait():
                tp_n[0] += 1
                dve.wait_ge(win["tp_full"], tp_n[0])

            def divide(w):
                g = w % NG
                tp_wait()
                link(nc.vector.reciprocal(rden[:], bank_tp[:, :, HD]))
                inv = rden[:].unsqueeze(2).to_broadcast([P, TC * NG, HD])
                if w < NG:
                    nc.vector.tensor_tensor(st8[:], bank_tp[:, :, 0:HD], inv, ALU.mult).then_inc(win["tp_read"], 1)
                    dve.wait_ge(win["tp_read"], tp_n[0])
                    link(nc.vector.tensor_copy(qstack[:, :, 0:HD].bitcast(F32R), st8[:]))
                    nc.vector.tensor_copy(qstack[:, :, HD:2 * HD], qstack[:, :, 0:HD])
                    nc.vector.tensor_tensor(qstack[:, :, 2 * HD:3 * HD].bitcast(F32R), st8[:], qstack[:, :, 0:HD],
                                            ALU.subtract).then_inc(win["state_ready"], 1)
                    return
                a = int(w >= W_FIRST)
                heads = O[a][:].rearrange("p c (h d) -> p c h d", d=HD)
                heads = heads[:, :, NG * g:NG * g + NG, :] if a == 0 else heads[:, :, g:NH:NG, :]
                nc.vector.tensor_tensor(heads, bank_tp[:, :, 0:HD].rearrange("p (c j) d -> p c j d", c=TC),
                                        inv.rearrange("p (c j) d -> p c j d", c=TC),
                                        ALU.mult).then_inc(win["tp_read"], 1)
                if w == W_FIRST - 1:
                    dve.wait_ge(win["tp_read"], tp_n[0])
                    dve.sem_inc(win["o0_ready"], 1)

            def slot_work(plan, w, u):
                if u == AT_ROWS_IN and w - 1 in plan.maxes:
                    dve.wait_ge(win["sm_read"], SLOTS * plan.max_rank(w))
                    nc.vector.tensor_copy(mx[:, :, ADD0:ROWS],
                                          negmax[:].rearrange("p c j -> p (c j)").unsqueeze(2)
                                          .to_broadcast([P, TC * NG, ROWS - ADD0])).then_inc(win["mx_ready"], 1)
                    dve.wait_ge(win["mx_ready"], plan.max_rank(w))
                if w in plan.maxes:
                    j, tc = u // TC, u % TC
                    unit = ("sm", w, u)
                    dve.wait_ge(win["sm_ready"], plan.number(unit) + 1)
                    nc.vector.tensor_reduce(negmax[:, tc, j:j + 1], ps[:, plan.bank(unit), :], AX_X, ALU.max,
                                            negate=True).then_inc(win["sm_read"], 1)
                if u == AT_SUMS and w - 1 in plan.active:
                    dve.wait_ge(win["pv_done"], TC * plan.rank(w))
                    nc.vector.tensor_copy(uts[:], ps[:, B_UT, :]).then_inc(win["ut_copied"], 1)
                if u == AT_DIVIDE and w - 1 in plan.active:
                    divide(w - 1)
                if u == AT_QUERY and w - 1 in plan.active and w - 1 < NG:
                    tp_wait()
                    nc.vector.tensor_copy(qT[0][:, (w - 1) * S:w * S], ps[:, B_TP, :]).then_inc(win["qt_ready"], 1)
                    dve.wait_ge(win["qt_ready"], w)
                    dve.sem_inc(win["tp_read"], 1)
                if u == AT_ROWS_OUT and w - 1 in plan.maxes:
                    a, g = MAX_AT[w - 1]
                    tp_wait()
                    rows = qT[a][:, g * S:(g + 1) * S]
                    nc.vector.tensor_tensor(rows, ps[:, B_TP, :], rows.bitcast(F32), ALU.add).then_inc(win["qm_ready"], 1)
                    dve.wait_ge(win["qm_ready"], plan.max_rank(w))
                    dve.sem_inc(win["tp_read"], 1)

            def start_second():
                dve.wait_ge(pre[1]["op_act"], copied(1, len(all_kinds(1)), 0))

            def turn(b, parts):
                steps[0] = tp_n[0] = 0
                run_turn(parts, slot_work, start_second, dense, experts, prelude, output)
                dve.drain().then_inc(turn_end, 1)
                dve.wait_ge(turn_go, b + 2)
                dve.sem_inc(turn_begun, 1)

            turns(dve, turn)

        @block.gpsimd
        def _(pool):
            def wide(tile):
                return tile[:].unsqueeze(1).to_broadcast([P, TC, P])

            def dense(k, early):
                yield from idle(0 if early else LN_STEPS)
                X = (x_next, x_a)[k]
                pool.wait_ge(ffn[k]["ln_ready"], TC)
                nc.gpsimd.tensor_tensor(X[:], X[:], wide(bffn), ALU.add).then_inc(ffn[k]["xb_ready"], 1)
                yield
                yield
                yield

            def output(a, early):
                yield
                yield
                yield

            def experts(k, early):
                yield from idle(LN_STEPS + 5 + GATE_STEPS + 2 * (len(UNITS) + 2) - 1)

            def prelude(a, early):
                s = pre[a]
                X = (x_next, x_b)[a]
                yield from idle((1 if a else 0 if early else 2) * LN_STEPS)
                if a == 0:
                    pool.wait_ge(s["x1_ready"], TC)
                    nc.gpsimd.tensor_tensor(X[:], X[:], R[:], ALU.add).then_inc(pool_step, 1)
                    pool.wait_ge(pool_step, 1)
                else:
                    pool.wait_ge(s["ln_ready"], TC)
                nc.gpsimd.tensor_tensor(X[:], X[:], wide(bo[a]), ALU.add).then_inc(s["res_ready"], 1)
                yield
                yield from idle(5 if a else 5 + INV_STEPS)
                for i, kind in enumerate(KINDS[a]):
                    if i:
                        pool.wait_ge(s["op_psum"], NG * i)
                    if kind == "v":
                        nc.gpsimd.memset(stack[:, :, HD:HD + 1], 1.0).then_inc(s["extra_ready"], 1)
                    else:
                        columns = extra[:, 2 * a + i, :].unsqueeze(1).to_broadcast([P, TC * NH, NJ])
                        nc.gpsimd.tensor_copy(stack[:, :, ADD0:ROWS], columns).then_inc(s["extra_ready"], 1)
                        off = 2 * HD if kind == "k" else HD
                        pool.wait_ge(s["hi_ready"], i + 1)
                        nc.gpsimd.tensor_copy(stack[:, :, off:off + HD], stack[:, :, 0:HD]).then_inc(s["dup_ready"], 1)
                    yield from idle(STACK_STEPS + NG + 1)
                if a == 1:
                    yield from idle(NG + 1)

            def turn(b, parts):
                run_turn(parts, lambda plan, w, u: None, lambda: None, dense, experts, prelude, output)
                pool.drain().then_inc(turn_end, 1)
                pool.wait_ge(turn_go, b + 2)
                pool.sem_inc(turn_begun, 1)

            turns(pool, turn)


def kernel(**inputs):
    import concourse.bacc as bacc
    from concourse.bass_utils import run_bass_kernel_spmd

    a = {k: np.asarray(v) for k, v in inputs.items()}

    def cat(*ws):
        return np.ascontiguousarray(np.concatenate(ws, axis=-1))

    w1 = np.concatenate([a["L1_ffn_w1"], a["L1_ffn_w1s"]], 0)
    w3 = np.concatenate([a["L1_ffn_w3"], a["L1_ffn_w3s"]], 0)
    w2 = np.concatenate([a["L1_ffn_w2"], a["L1_ffn_w2s"]], 0)
    w13 = np.stack([w1, w3], 1).transpose(2, 0, 1, 3).reshape(P, -1)

    own = (np.arange(P) % ROWS) // TOKENS_OF_BLOCK
    blocks = np.arange(NJ)
    static = (np.abs(own[:, None] - blocks) <= 1) | (blocks == 0) | (blocks == NJ - 1)
    consts = np.concatenate([static, own[:, None] == blocks, np.tile(blocks, (P, 1)), own[:, None]], 1)

    arrays = {
        "x": a["L0_attn_hidden_states"],
        "ffn_wT": a["L0_ffn_W"].T, "ffn_vT": a["L0_ffn_V_r"].T, "ffn_cT": a["L0_ffn_C"].T, "ffn_b": a["L0_ffn_b"],
        "wqkv0": cat(a["L0_attn_Wq"], a["L0_attn_Wk"], a["L0_attn_Wv"]),
        "bqkv0": cat(a["L0_attn_bq"], a["L0_attn_bk"], a["L0_attn_bv"]),
        "wo0": a["L0_attn_Wo"], "bo0": a["L0_attn_bo"],
        "lnw": a["L0_attn_ln_w"][:, None], "lnb": a["L0_attn_ln_b"][:, None],
        "wqkv1": cat(a["L1_attn_Wq"].T, a["L1_attn_Wk"].T, a["L1_attn_Wv"].T),
        "bqkv1": cat(a["L1_attn_bq"], a["L1_attn_bk"], a["L1_attn_bv"]),
        "wo1": a["L1_attn_Wo"].T, "bo1": a["L1_attn_bo"],
        "src": a["L1_attn_src_blocks"], "tgt": a["L1_attn_tgt_blocks"],
        "gateT": a["L1_ffn_gate_w"].T, "w13": w13, "w2": w2.transpose(1, 0, 2),
        "ident": np.eye(P, dtype=np.float32), "consts": consts.astype(np.float32),
    }
    arrays = {k: np.ascontiguousarray(v) for k, v in arrays.items()}
    nc = bacc.Bacc("TRN2", target_bir_lowering=False, num_devices=1)
    args = {k: nc.dram_tensor(f"in_{k}", v.shape, mybir.dt.from_np(v.dtype), kind="ExternalInput").ap()
            for k, v in arrays.items()}
    shape = arrays["x"].shape
    args["out"] = nc.dram_tensor("out_0", shape, F32, kind="ExternalOutput").ap()
    build(nc, **args)
    r = run_bass_kernel_spmd(nc, [{f"in_{k}": v for k, v in arrays.items()}], core_ids=[0])
    return r.results[0]["out_0"]
```
